# Optimizing a Trainium2 kernel written in Bass

```python
import numpy as np
import jax
import jax.numpy as jnp

def _softmax(x, axis=-1):
    return jax.nn.softmax(x, axis=axis)

def _gelu(x):
    return jax.nn.gelu(x, approximate=True)

def _silu(x):
    return jax.nn.silu(x)

def _sigmoid(x):
    return jax.nn.sigmoid(x)

def _layernorm(x, axis=-1, eps=1e-05):
    m = jnp.mean(x, axis=axis, keepdims=True)
    v = jnp.var(x, axis=axis, keepdims=True)
    return (x - m) / jnp.sqrt(v + eps)

def _scatter_add(tgt, idx, src, axis=0):
    return tgt.at[idx].add(src)

def _segment_sum(src, seg, n):
    return jax.ops.segment_sum(src, seg, n)
kernel_name = 'mk_gnn_preln_d1_gnn_r32_abf1c4'

def setup_inputs(seed: int=0):
    np.random.seed(seed)
    _w = jnp.asarray

    def _rec_inputs():
        import jax
        import jax.numpy as jnp
        _gk = jax.random.key(seed)
        x = -0.0009044 + 1 * jax.random.normal(jax.random.fold_in(_gk, 1), (3125, 160), jnp.float32)
        _s = jax.random.randint(jax.random.fold_in(_gk, 2), (25000,), 0, 3125, jnp.int32)
        _d = jax.random.randint(jax.random.fold_in(_gk, 3), (25000,), 0, 3125, jnp.int32)
        _loop = jnp.arange(3125, dtype=jnp.int32)
        src = jnp.concatenate([_s, _d, _loop])
        dst = jnp.concatenate([_d, _s, _loop])
        _o = jnp.argsort(dst, stable=True)
        src = src[_o]
        dst = dst[_o]
        edge_attr_3 = 0.00047201 + 1.00023 * jax.random.normal(jax.random.fold_in(_gk, 11), (53125, 3), jnp.float32)
        edge_attr_64 = 0.000279952 + 1.00013 * jax.random.normal(jax.random.fold_in(_gk, 12), (53125, 64), jnp.float32)
        return (x, src, dst, edge_attr_3, edge_attr_64)
    x, src, dst, edge_attr_3, edge_attr_64 = _rec_inputs()

    def _L0_gnn_setup():
        import jax, jax.numpy as jnp
        import numpy as np
        N_NODES = 10000
        N_EDGES = 10000
        MUL0, MUL1 = (64, 32)
        EDGE_DIM = 64
        W_NUMEL = 224
        DENOM = 32.0
        SQRT3 = 3.0 ** 0.5
        INV_SQRT3 = 1.0 / SQRT3
        INV_SQRT2 = 2.0 ** (-0.5)

        def _forward(node_feature, edge_attr, edge_feature, W_skip0, W_skip1, W_nl0, W_nl1, W_fc1, W_fc2, W_out_s, W_out_v, edge_index):
            N = node_feature.shape[0]
            E = edge_attr.shape[0]
            s = node_feature[:, :MUL0]
            v = node_feature[:, MUL0:].reshape(N, MUL1, 3)
            skip_s = s @ W_skip0
            skip_v = jnp.einsum('nmi,mk->nki', v, W_skip1)
            s = s @ W_nl0
            v = jnp.einsum('nmi,mk->nki', v, W_nl1)
            rhat = edge_attr / jnp.linalg.norm(edge_attr, axis=-1, keepdims=True)
            sh1 = SQRT3 * rhat
            w = jax.nn.relu(edge_feature @ W_fc1) @ W_fc2
            w0, w1, w2, w3, w4 = jnp.split(w, [64, 128, 160, 192], axis=-1)
            src, dst = (edge_index[0], edge_index[1])
            xs = s[dst]
            xv = v[dst]
            out0a = w0 * xs
            out0b = w3 * (jnp.einsum('emi,ei->em', xv, sh1) * INV_SQRT3)
            out1a = (w1 * xs)[:, :, None] * sh1[:, None, :]
            out1b = w2[:, :, None] * xv
            out1c = w4[:, :, None] * (jnp.cross(xv, sh1[:, None, :]) * INV_SQRT2)
            tp = jnp.concatenate([out0a, out0b, out1a.reshape(E, -1), out1b.reshape(E, -1), out1c.reshape(E, -1)], axis=-1)
            agg = jax.ops.segment_sum(tp, src, num_segments=N) / DENOM
            agg_s = agg[:, :96]
            agg_v = agg[:, 96:].reshape(N, 128, 3)
            out_s = agg_s @ W_out_s + skip_s
            out_v = jnp.einsum('nmi,mk->nki', agg_v, W_out_v) + skip_v
            fs = jax.nn.silu(out_s[:, :MUL0])
            gate = jax.nn.sigmoid(out_s[:, MUL0:MUL0 + 32])
            gv = gate[:, :, None] * out_v
            return jnp.concatenate([fs, gv.reshape(N, -1)], axis=-1)
        key = jax.random.key(seed)
        ks = jax.random.split(key, 12)

        def lin(k, fi, fo):
            return jax.random.normal(k, (fi, fo), jnp.float32) / np.float32(np.sqrt(fi))
        return {'node_feature': jax.random.normal(ks[0], (N_NODES, MUL0 + 3 * MUL1), jnp.float32), 'edge_attr': jax.random.normal(ks[1], (N_EDGES, 3), jnp.float32), 'edge_feature': jax.random.normal(ks[2], (N_EDGES, EDGE_DIM), jnp.float32), 'W_skip0': lin(ks[3], MUL0, 96), 'W_skip1': lin(ks[4], MUL1, 32), 'W_nl0': lin(ks[5], MUL0, MUL0), 'W_nl1': lin(ks[6], MUL1, MUL1), 'W_fc1': lin(ks[7], EDGE_DIM, 64), 'W_fc2': lin(ks[8], 64, W_NUMEL), 'W_out_s': lin(ks[9], 96, 96), 'W_out_v': lin(ks[10], 128, 32), 'edge_index': jax.random.randint(ks[11], (2, N_EDGES), 0, N_NODES)}
    _L0_gnn_all = _L0_gnn_setup()
    _L0_gnn_in = {k: v for k, v in _L0_gnn_all.items() if k in ('W_skip0', 'W_skip1', 'W_nl0', 'W_nl1', 'W_fc1', 'W_fc2', 'W_out_s', 'W_out_v')}
    del _L0_gnn_all
    return {'x': x, 'src': src, 'dst': dst, 'edge_attr_3': edge_attr_3, 'edge_attr_64': edge_attr_64, 'L0_gnn_W_skip0': _L0_gnn_in['W_skip0'], 'L0_gnn_W_skip1': _L0_gnn_in['W_skip1'], 'L0_gnn_W_nl0': _L0_gnn_in['W_nl0'], 'L0_gnn_W_nl1': _L0_gnn_in['W_nl1'], 'L0_gnn_W_fc1': _L0_gnn_in['W_fc1'], 'L0_gnn_W_fc2': _L0_gnn_in['W_fc2'], 'L0_gnn_W_out_s': _L0_gnn_in['W_out_s'], 'L0_gnn_W_out_v': _L0_gnn_in['W_out_v']}

def reference(x, src, dst, edge_attr_3, edge_attr_64, L0_gnn_W_skip0, L0_gnn_W_skip1, L0_gnn_W_nl0, L0_gnn_W_nl1, L0_gnn_W_fc1, L0_gnn_W_fc2, L0_gnn_W_out_s, L0_gnn_W_out_v):
    import jax
    import jax.numpy as jnp

    def _L0_gnn_ref(node_feature, edge_attr, edge_feature, W_skip0, W_skip1, W_nl0, W_nl1, W_fc1, W_fc2, W_out_s, W_out_v, edge_index):
        import jax, jax.numpy as jnp
        import numpy as np
        N_NODES = 10000
        N_EDGES = 10000
        MUL0, MUL1 = (64, 32)
        EDGE_DIM = 64
        W_NUMEL = 224
        DENOM = 32.0
        SQRT3 = 3.0 ** 0.5
        INV_SQRT3 = 1.0 / SQRT3
        INV_SQRT2 = 2.0 ** (-0.5)

        def _forward(node_feature, edge_attr, edge_feature, W_skip0, W_skip1, W_nl0, W_nl1, W_fc1, W_fc2, W_out_s, W_out_v, edge_index):
            N = node_feature.shape[0]
            E = edge_attr.shape[0]
            s = node_feature[:, :MUL0]
            v = node_feature[:, MUL0:].reshape(N, MUL1, 3)
            skip_s = s @ W_skip0
            skip_v = jnp.einsum('nmi,mk->nki', v, W_skip1)
            s = s @ W_nl0
            v = jnp.einsum('nmi,mk->nki', v, W_nl1)
            rhat = edge_attr / jnp.linalg.norm(edge_attr, axis=-1, keepdims=True)
            sh1 = SQRT3 * rhat
            w = jax.nn.relu(edge_feature @ W_fc1) @ W_fc2
            w0, w1, w2, w3, w4 = jnp.split(w, [64, 128, 160, 192], axis=-1)
            src, dst = (edge_index[0], edge_index[1])
            xs = s[dst]
            xv = v[dst]
            out0a = w0 * xs
            out0b = w3 * (jnp.einsum('emi,ei->em', xv, sh1) * INV_SQRT3)
            out1a = (w1 * xs)[:, :, None] * sh1[:, None, :]
            out1b = w2[:, :, None] * xv
            out1c = w4[:, :, None] * (jnp.cross(xv, sh1[:, None, :]) * INV_SQRT2)
            tp = jnp.concatenate([out0a, out0b, out1a.reshape(E, -1), out1b.reshape(E, -1), out1c.reshape(E, -1)], axis=-1)
            agg = jax.ops.segment_sum(tp, src, num_segments=N) / DENOM
            agg_s = agg[:, :96]
            agg_v = agg[:, 96:].reshape(N, 128, 3)
            out_s = agg_s @ W_out_s + skip_s
            out_v = jnp.einsum('nmi,mk->nki', agg_v, W_out_v) + skip_v
            fs = jax.nn.silu(out_s[:, :MUL0])
            gate = jax.nn.sigmoid(out_s[:, MUL0:MUL0 + 32])
            gv = gate[:, :, None] * out_v
            return jnp.concatenate([fs, gv.reshape(N, -1)], axis=-1)
        return _forward(node_feature, edge_attr, edge_feature, W_skip0, W_skip1, W_nl0, W_nl1, W_fc1, W_fc2, W_out_s, W_out_v, edge_index)
    edge_index = jnp.stack([src, dst])
    h = jnp.maximum(_layernorm(x, axis=-1), 0.0)
    x = x + _L0_gnn_ref(h, edge_attr_3, edge_attr_64, L0_gnn_W_skip0, L0_gnn_W_skip1, L0_gnn_W_nl0, L0_gnn_W_nl1, L0_gnn_W_fc1, L0_gnn_W_fc2, L0_gnn_W_out_s, L0_gnn_W_out_v, edge_index)
    return x

_drawn_inputs = setup_inputs


def setup_inputs(seed=0):
    import zlib

    import numpy as np

    out = dict(_drawn_inputs(seed))
    spreads = {}
    factors = {}
    for name, (base, spread) in spreads.items():
        noise = np.random.default_rng([zlib.crc32(name.encode()), seed]).standard_normal(out[name].shape)
        drawn = base * np.exp(spread * noise) if base else spread * noise
        out[name] = jnp.asarray(drawn.astype(out[name].dtype))
    for name, factor in factors.items():
        out[name] = (out[name] * factor).astype(out[name].dtype)
    return out
```

```python
from contextlib import ExitStack

import numpy as np

import concourse.bass as bass
from concourse import mybir

ALU = mybir.AluOpType
ACT = mybir.ActivationFunctionType
AXX = mybir.AxisListType.X
F32 = mybir.dt.float32
I32 = mybir.dt.int32

P = 128
N = 3125
E = 53125
S, V = 64, 32
F = S + 3 * V
FE = 64
NT = -(-N // P)
NPAD = NT * P
TILES = 416
HALF = TILES // 2
J = 4
GROUPS = TILES // J
BLOCKS = GROUPS // 2
UNROLL = 4
GE = J * P
SO = S + V
M = SO + 3 * V
TABLE_ROWS = NPAD + P
DOT, SC, VE, CR, G_END = 0, V, V + S, V + S + 3 * V, V + S + 6 * V
CHUNKS = ((DOT, VE), (SC, VE + 2 * V), (VE + 2 * V, G_END))
ROWS = tuple(b - a for a, b in CHUNKS)
Q = M
OUTS = M + V
NR = SO
NV = SO + F
NALL = NV + 3 * V
CH = 5
EPS = 1e-5

W_FC1 = 0
W_FC2 = W_FC1 + P
W_MA = W_FC2 + sum(ROWS)
W_MB = W_MA + SO
W_MC = W_MB + 3 * V
W_NS = W_MC + 3 * V
W_NV = W_NS + SO + S
W_ID = W_NV + 6 * V
W_LT = W_ID + P
W_DUMP = W_LT + P
W_END = W_DUMP + 1


def valid(k, n):
    return not isinstance(k, int) or 0 <= k < n


def build_program(nc, x, wpack, edge_t, nodes_to, nodes_from, nodes_row, edge_vec, out):
    table = nc.dram_tensor("node_table", [NPAD, F], F32, kind="Internal").ap()
    sums = [nc.dram_tensor(f"sums_{j}", [TABLE_ROWS, M], F32, kind="Internal").ap() for j in range(J)]

    with ExitStack() as ctx:
        def sb(name, shape, dt=F32):
            return ctx.enter_context(nc.sbuf_tensor(name, shape, dt))

        def ps(name, shape):
            return ctx.enter_context(nc.psum_tensor(name, shape, F32))

        def sem(name):
            return ctx.enter_context(nc.semaphore(name))

        w = sb("w", [P, W_END])
        ident = w[:, W_ID:W_ID + P]
        lower = w[:, W_LT:W_LT + P]
        x_sb = sb("x_sb", [P, NT, F])
        xc = sb("xc", [P, NT, F])
        nodes = sb("nodes", [P, NT, NALL])
        stat = sb("stat", [P, 4, NT])
        hT = sb("hT", [P, 2, 2, P])
        zeros = sb("zeros", [P, TABLE_ROWS // P, M])
        rhat = sb("rhat", [P, TILES, 5])
        vec = sb("vec", [P, TILES, 3])[:, :, :]
        vec_sq = xc[:, :, :].rearrange("p a b -> p (a b)")[:, 0:TILES * 3].rearrange("p (t c) -> p t c", c=3)
        vlen = sb("vlen", [P, 2, TILES])
        cst = sb("cst", [P, 1])

        ef = sb("ef", [P, 2, GE])
        to_idx = sb("to_idx", [P, 2, 2 * J], I32)
        from_col = sb("from_col", [P, 2, 2 * J], I32)
        from_row = sb("from_row", [P, 2, 2 * GE], I32)
        hid = sb("hid", [P, 2, GE])
        rows = sb("rows", [P, UNROLL, J, G_END])
        G = [rows[:, u] for u in range(UNROLL)]
        wT = [[sb(f"wT{c}{k}", [ROWS[c], GE]) for k in range(2)] for c in range(3)]
        pT = [[sb(f"pT{c}{k}", [ROWS[c], GE]) for k in range(2)] for c in range(3)]
        crs = sb("crs", [P, 3, J, 3 * V])
        msg = sb("msg", [P, 2, J, OUTS])
        radial = sb("radial", [P, 2, 2, 3 * V])
        same = sb("same", [P, 2, J, P])
        before = sb("before", [P, 2, J, P])
        key = sb("key", [P, 3, 2, J])
        to_add = sb("to_add", [P, UNROLL, J, M])
        add_idx = sb("add_idx", [P, UNROLL, J], I32)

        hid_ps = ps("hid_ps", [P, GE])
        w_ps = [ps(f"w_ps{k}", [P, GE]) for k in range(2)]
        x_ps = [ps(f"x_ps{k}", [P, GE]) for k in range(2)]
        o_ps = [ps(f"o_ps{k}", [P, GE]) for k in range(2)]
        d_ps = ps("d_ps", [P, GE])

        w_in, x_in, vec_in = sem("w_in"), sem("x_in"), sem("vec_in")
        passed = sem("passed")
        zero_set, zeroed = sem("zero_set"), sem("zeroed")
        scaled = sem("scaled")
        vstep, astep = sem("vstep"), sem("astep")
        normed, turned, turned_sb, projected, nodes_ready = (
            sem(n) for n in ("normed", "turned", "turned_sb", "projected", "nodes_ready"))
        table_out = sem("table_out")
        rhat_ready = sem("rhat_ready")
        edges_in = [sem(f"edges_in{k}") for k in range(2)]
        to_in = [sem(f"to_in{k}") for k in range(2)]
        gathered = [sem(f"gathered{u}") for u in range(UNROLL)]
        products, crossed = sem("products"), sem("crossed")
        fc1_done, hid_ready = sem("fc1_done"), sem("hid_ready")
        fc2_done, w_ready = sem("fc2_done"), sem("w_ready")
        x_turned, prod_ready = sem("x_turned"), sem("prod_ready")
        out_done, out_copied, radial_ready, msg_ready = (
            sem(n) for n in ("out_done", "out_copied", "radial_ready", "msg_ready"))
        keys, repeats_ready, same_ready, idx_ready = sem("keys"), sem("repeats_ready"), sem("same_ready"), sem("idx_ready")
        summed, sums_ready, added = sem("summed"), sem("sums_ready"), sem("added")
        parts_in = [sem(f"parts_in{k}") for k in range(2)]
        total_ready, gate_ready, out_ready, stored = (
            sem(n) for n in ("total_ready", "gate_ready", "out_ready", "stored"))

        x_d = x.rearrange("(p t) f -> p t f", t=NT)
        out_d = out.rearrange("(p t) f -> p t f", t=NT)
        table_d = table.rearrange("(p t) f -> p t f", t=NT)
        sums_d = [s[0:NPAD, :].rearrange("(p t) m -> p t m", t=NT) for s in sums]
        squares = rows[:, :, :, :].rearrange("p u j f -> p (u j f)")[:, 0:NT * F].rearrange("p (t f) -> p t f", f=F)
        part = [flat[:, 0:J * CH * M].rearrange("p (j t m) -> p j t m", j=J, t=CH)
                for flat in (xc[:, :, :].rearrange("p a b -> p (a b)"),
                             rows[:, :, :, :].rearrange("p u j f -> p (u j f)"))]

        block = ctx.enter_context(nc.Block())

        @block.sync
        def _(sp):
            sp.dma_start(w[:], wpack).then_inc(w_in, 16)
            sp.dma_start(vec, edge_vec).then_inc(vec_in, 16)
            for c in range(NT // CH):
                sp.dma_start(x_sb[:, c * CH:(c + 1) * CH, :], x_d[:, c * CH:(c + 1) * CH, :]).then_inc(x_in, 16)

            def load_edges(b, par):
                if valid(b - 2, BLOCKS):
                    sp.wait_ge(idx_ready, 2 * b - 2)
                sp.dma_start(ef[:, par, :], edge_t[:, bass.ds(b * GE, GE)]).then_inc(edges_in[par], 16)
                sp.dma_start(from_col[:, par, :], nodes_from[:, bass.ds(b * 2 * J, 2 * J)]).then_inc(edges_in[par], 16)
                sp.dma_start(from_row[:, par, :],
                             nodes_row[:, bass.ds(b * 2 * GE, 2 * GE)].partition_broadcast(P)
                             ).then_inc(edges_in[par], 16)

            def load_to(b, par):
                if valid(b - 2, BLOCKS):
                    sp.wait_ge(gathered[2 * par + 1], 16 * J * (b // 2) if isinstance(b, int) else 16 * J * b_half[0])
                sp.dma_start(to_idx[:, par, :], nodes_to[:, bass.ds(b * 2 * J, 2 * J)]).then_inc(to_in[par], 16)

            b_half = [None]
            for b in range(2):
                load_to(b, b)
                load_edges(b, b)

            for c in range(NT // CH):
                sp.wait_ge(nodes_ready, (c + 1) * CH)
                sp.dma_start(table_d[:, c * CH:(c + 1) * CH, :],
                             nodes[:, c * CH:(c + 1) * CH, NR:NR + F]).then_inc(table_out, 16)

            with sp.Fori(1, BLOCKS // 2) as i:
                b_half[0] = i
                for par in range(2):
                    load_to(2 * i + par, par)
                    load_edges(2 * i + par, par)

            sp.wait_ge(added, 16 * J * GROUPS)
            for c in range(NT // CH):
                if c >= 2:
                    sp.wait_ge(total_ready, c - 1)
                for j in range(J):
                    sp.dma_start(part[c % 2][:, j], sums_d[j][:, c * CH:(c + 1) * CH, :]).then_inc(parts_in[c % 2], 16)
            for c in range(NT // CH):
                sp.wait_ge(out_ready, c + 1)
                sp.dma_start(out_d[:, c * CH:(c + 1) * CH, :], x_sb[:, c * CH:(c + 1) * CH, :]).then_inc(stored, 16)
            sp.wait_ge(stored, 16 * (NT // CH))

        @block.gpsimd
        def _(pool):
            nc.gpsimd.memset(zeros[:], 0.0).then_inc(zero_set, 1)

            def tick():
                pool.sem_inc(passed, 1)

            def gather(g, u, i):
                if not valid(g, GROUPS):
                    return
                par, h = u // 2, u % 2
                if h == 0:
                    pool.wait_ge(to_in[par], 16 * (i + 1))
                if valid(g - UNROLL, GROUPS):
                    pool.wait_ge(x_turned, 3 * (g - UNROLL + 1))
                    tick()
                else:
                    pool.wait_ge(table_out, 16 * (NT // CH))
                for j in range(J):
                    pool.indirect_dma_start(
                        G[u][:, j, SC:CR], None, table,
                        bass.IndirectOffsetOnAxis(ap=to_idx[:, par, h * J + j:h * J + j + 1], axis=0),
                    ).then_inc(gathered[u], 16)

            def scatter(g, u):
                if not valid(g, GROUPS):
                    return
                pool.wait_ge(sums_ready, 2 * g + 2)
                pool.wait_ge(idx_ready, g + 1)
                if valid(g - 1, GROUPS):
                    pool.wait_ge(added, 16 * J * g)
                    tick()
                else:
                    pool.wait_ge(zeroed, 16 * J)
                for j in range(J):
                    pool.indirect_dma_start(
                        sums[j], bass.IndirectOffsetOnAxis(ap=add_idx[:, u, j:j + 1], axis=0),
                        to_add[:, u, j, :], None, compute_op=ALU.add,
                    ).then_inc(added, 16)

            def steps(i):
                for u in range(UNROLL):
                    g = UNROLL * i + u
                    gather(g + 2, (u + 2) % UNROLL, i + (u + 2) // UNROLL)
                    scatter(g - 2, (u - 2) % UNROLL)

            gather(0, 0, 0)
            gather(1, 1, 0)
            steps(0)
            with pool.Fori(1, GROUPS // UNROLL - 1) as i:
                steps(i)
            steps(GROUPS // UNROLL - 1)
            scatter(GROUPS - 2, 2)
            scatter(GROUPS - 1, 3)

        @block.tensor
        def _(pe):
            pe.wait_ge(w_in, 16)
            for t in range(NT):
                k = t % 2
                hp, op = x_ps[k], o_ps[k]
                if t % CH == 0:
                    pe.wait_ge(normed, t // CH + 1)
                if t >= 2:
                    pe.wait_ge(turned_sb, t - 1)
                nc.tensor.transpose(hp[0:S, 0:P], xc[:, t, 0:S], ident)
                nc.tensor.transpose(hp[0:3 * V, P:2 * P],
                                    xc[:, t, S:F], ident).then_inc(turned, 1)
                pe.wait_ge(turned_sb, t + 1)
                if t >= 2:
                    pe.wait_ge(nodes_ready, t - 1)
                nc.tensor.matmul(op[:, 0:SO + S], hT[0:S, k, 0, :], w[0:S, W_NS:W_NS + SO + S],
                                 start=True, stop=False, skip_group_check=True)
                nc.tensor.matmul(op[:, SO + S:SO + S + 6 * V], hT[0:3 * V, k, 1, :], w[0:3 * V, W_NV:W_NV + 6 * V],
                                 start=False, stop=True, skip_group_check=True).then_inc(projected, 1)

            def fc1(b, par, i):
                if not valid(b, BLOCKS):
                    return
                pe.wait_ge(edges_in[par], 48 * (i + 1))
                if valid(b - 1, BLOCKS):
                    pe.wait_ge(hid_ready, b)
                nc.tensor.matmul(hid_ps[:], w[:, W_FC1:W_FC1 + P], ef[:, par, :],
                                 start=True, stop=True).then_inc(fc1_done, 1)

            def fc2(g, u, c):
                par, h = u // 2, u % 2
                kk = (3 * u + c) % 2
                if c == 0 and h == 0:
                    pe.wait_ge(hid_ready, (g + 2) // 2 if isinstance(g, int) else half_block(g, u) + 1)
                if valid(g - 1, GROUPS) or c == 2:
                    pe.wait_ge(w_ready, 3 * g + c - 1)
                at = W_FC2 + sum(ROWS[:c])
                nc.tensor.matmul(w_ps[kk][0:ROWS[c], :], w[FE * h:FE * h + FE, at:at + ROWS[c]],
                                 hid[FE * h:FE * h + FE, par, :], start=True, stop=True).then_inc(fc2_done, 1)

            def turn(g, u, c):
                kk = (3 * u + c) % 2
                if c == 0:
                    pe.wait_ge(crossed, g + 1)
                if valid(g - 1, GROUPS) or c == 2:
                    pe.wait_ge(prod_ready, 3 * g + c - 1)
                a, e = CHUNKS[c]
                for j in range(J):
                    ins = nc.tensor.transpose(x_ps[kk][0:ROWS[c], j * P:(j + 1) * P], G[u][:, j, a:e], ident)
                ins.then_inc(x_turned, 1)

            def outputs(g, u, m):
                if not valid(g, GROUPS):
                    return
                if m == 0:
                    pe.wait_ge(prod_ready, 3 * g + 3)
                if valid(g - 1, GROUPS):
                    pe.wait_ge(out_copied, 2 * g + m - 1)
                for q in range(2):
                    cols = slice((2 * m + q) * P, (2 * m + q + 1) * P)
                    base = q * OUTS
                    for c, (wc, oc, n) in enumerate(((W_MA, 0, SO), (W_MB, SO + V, 3 * V), (W_MC, SO, 3 * V))):
                        ins = nc.tensor.matmul(o_ps[m][:, base + oc:base + oc + n], pT[c][u % 2][:, cols],
                                               w[0:ROWS[c], wc:wc + n], start=(q == 0 and c == 0),
                                               stop=(q == 1 and c == 2), skip_group_check=True)
                ins.then_inc(out_done, 1)

            def merge(g, u, m):
                if not valid(g, GROUPS):
                    return
                pe.wait_ge(msg_ready, 2 * g + m + 1)
                if m == 0:
                    pe.wait_ge(same_ready, g + 1)
                if valid(g - 1, GROUPS) or m == 1:
                    pe.wait_ge(sums_ready, 2 * g + m)
                for q in range(2):
                    ins = nc.tensor.matmul(d_ps[:, q * M:(q + 1) * M], same[:, u % 2, 2 * m + q, :],
                                           msg[:, u % 2, 2 * m + q, 0:M], start=(q == 0), stop=(q == 1),
                                           skip_group_check=True)
                ins.then_inc(summed, 1)

            loop = [0]

            def half_block(g, u):
                return 2 * loop[0] + u // 2

            def step(i, u):
                g = UNROLL * i + u
                v = (u - 1) % UNROLL
                fc2(g, u, 0)
                turn(g, u, 0)
                outputs(g - 1, v, 0)
                fc2(g, u, 1)
                turn(g, u, 1)
                outputs(g - 1, v, 1)
                if u % 2 == 1:
                    fc1(2 * i + u // 2 + 1, (u // 2 + 1) % 2, i + u // 3)
                fc2(g, u, 2)
                turn(g, u, 2)
                merge(g - 1, v, 0)
                merge(g - 1, v, 1)

            def steps(i):
                loop[0] = i
                for u in range(UNROLL):
                    step(i, u)

            fc1(0, 0, 0)
            steps(0)
            with pe.Fori(1, GROUPS // UNROLL - 1) as i:
                steps(i)
            steps(GROUPS // UNROLL - 1)
            for m in range(2):
                outputs(GROUPS - 1, 3, m)
            for m in range(2):
                merge(GROUPS - 1, 3, m)

        @block.scalar
        def _(act):
            act.wait_ge(zero_set, 1)
            for j in range(J):
                act.dma_start(sums[j].rearrange("(p t) m -> p t m", p=P), zeros[:]).then_inc(zeroed, 16)
            act.wait_ge(vstep, 1)
            nc.scalar.activation(vlen[:, 1, :], vlen[:, 0, :], ACT.Sqrt).then_inc(astep, 1)
            act.wait_ge(vstep, 2)
            nc.scalar.activation(stat[:, 2, :], stat[:, 1, :], ACT.Sqrt, bias=cst[:, 0:1],
                                 scale=1.0 / F).then_inc(astep, 1)
            for t in range(NT):
                if t % CH == 0:
                    act.wait_ge(vstep, 3)
                ins = nc.scalar.activation(xc[:, t, :], xc[:, t, :], ACT.Relu, scale=stat[:, 3, t:t + 1])
                if t % CH == CH - 1:
                    ins.then_inc(normed, 1)
            for t in range(NT):
                act.wait_ge(projected, t + 1)
                nc.scalar.activation(nodes[:, t, :], o_ps[t % 2][:, 0:NALL], ACT.Copy).then_inc(nodes_ready, 1)

            def hidden(b, par):
                if not valid(b, BLOCKS):
                    return
                act.wait_ge(fc1_done, b + 1)
                if valid(b - 2, BLOCKS):
                    act.wait_ge(fc2_done, 6 * b - 6)
                nc.scalar.activation(hid[:, par, :], hid_ps[:], ACT.Relu).then_inc(hid_ready, 1)

            def weights(g, u, c):
                act.wait_ge(fc2_done, 3 * g + c + 1)
                if valid(g - 2, GROUPS):
                    act.wait_ge(prod_ready, 3 * g + c - 5)
                nc.scalar.activation(wT[c][u % 2][:], w_ps[(3 * u + c) % 2][0:ROWS[c], :],
                                     ACT.Copy).then_inc(w_ready, 1)

            def copy_outputs(g, u, m):
                if not valid(g, GROUPS):
                    return
                act.wait_ge(out_done, 2 * g + m + 1)
                if valid(g - 2, GROUPS):
                    act.wait_ge(summed, 2 * g + m - 3)
                nc.scalar.activation(msg[:, u % 2, 2 * m:2 * m + 2, :],
                                     o_ps[m][:, 0:2 * OUTS].rearrange("p (q o) -> p q o", q=2),
                                     ACT.Copy).then_inc(out_copied, 1)

            def collect(g, u, m):
                if not valid(g, GROUPS):
                    return
                act.wait_ge(summed, 2 * g + m + 1)
                if valid(g - UNROLL, GROUPS):
                    act.wait_ge(added, 16 * J * (g - UNROLL + 1))
                nc.scalar.activation(to_add[:, u, 2 * m:2 * m + 2, :],
                                     d_ps[:, 0:2 * M].rearrange("p (q o) -> p q o", q=2),
                                     ACT.Copy).then_inc(sums_ready, 1)

            def step(i, u):
                g = UNROLL * i + u
                v = (u - 1) % UNROLL
                weights(g, u, 0)
                copy_outputs(g - 1, v, 0)
                weights(g, u, 1)
                copy_outputs(g - 1, v, 1)
                if u % 2 == 1:
                    hidden(2 * i + u // 2 + 1, (u // 2 + 1) % 2)
                weights(g, u, 2)
                collect(g - 1, v, 0)
                collect(g - 1, v, 1)

            hidden(0, 0)
            for u in range(UNROLL):
                step(0, u)
            with act.Fori(1, GROUPS // UNROLL - 1) as i:
                for u in range(UNROLL):
                    step(i, u)
            for u in range(UNROLL):
                step(GROUPS // UNROLL - 1, u)
            copy_outputs(GROUPS - 1, 3, 0)
            copy_outputs(GROUPS - 1, 3, 1)
            collect(GROUPS - 1, 3, 0)
            collect(GROUPS - 1, 3, 1)

            for c in range(NT // CH):
                act.wait_ge(total_ready, c + 1)
                nc.scalar.activation(zeros[:, c * CH:(c + 1) * CH, 0:SO], nodes[:, c * CH:(c + 1) * CH, 0:SO],
                                     ACT.Sigmoid).then_inc(gate_ready, 1)

        @block.vector
        def _(dve):
            nc.vector.memset(cst[:], EPS)
            dve.wait_ge(vec_in, 16)
            nc.vector.tensor_tensor(vec_sq, vec, vec, ALU.mult).then_inc(keys, 1)
            dve.wait_ge(keys, 1)
            nc.vector.tensor_reduce(vlen[:, 0, :], vec_sq, AXX, ALU.add).then_inc(vstep, 1)
            dve.wait_ge(astep, 1)
            nc.vector.reciprocal(vlen[:, 0, :], vlen[:, 1, :]).then_inc(keys, 1)
            dve.wait_ge(keys, 2)
            for a, n in ((0, 3), (3, 2)):
                nc.vector.tensor_tensor(rhat[:, :, a:a + n], vec[:, :, 0:n],
                                        vlen[:, 0, :].unsqueeze(2).broadcast_to([P, TILES, n]),
                                        ALU.mult).then_inc(rhat_ready, 1)
            dve.wait_ge(x_in, 16 * (NT // CH))
            nc.vector.tensor_reduce(stat[:, 0, :], x_sb[:], AXX, ALU.add).then_inc(keys, 1)
            dve.wait_ge(keys, 3)
            nc.vector.tensor_scalar(stat[:, 0, :], stat[:, 0, :], 1.0 / F, None, ALU.mult).then_inc(keys, 1)
            dve.wait_ge(keys, 4)
            nc.vector.tensor_tensor(xc[:], x_sb[:], stat[:, 0, :].unsqueeze(2).broadcast_to([P, NT, F]),
                                    ALU.subtract).then_inc(keys, 1)
            dve.wait_ge(keys, 5)
            nc.vector.tensor_tensor(squares, xc[:], xc[:], ALU.mult).then_inc(keys, 1)
            dve.wait_ge(keys, 6)
            nc.vector.tensor_reduce(stat[:, 1, :], squares, AXX, ALU.add).then_inc(vstep, 1)
            dve.wait_ge(w_in, 16)
            for r0 in range(0, P, V):
                for wc, n, scale in ((W_MA, SO, 1.0), (W_MB, 3 * V, 3 ** 0.5 if r0 < S else 1.0),
                                     (W_MC, 3 * V, 1.0 if r0 < V else 1.5 ** 0.5)):
                    if wc == W_MA and r0 >= SO:
                        continue
                    ins = nc.vector.tensor_scalar(w[r0:r0 + V, wc:wc + n], w[r0:r0 + V, wc:wc + n],
                                                  scale / 32.0, None, ALU.mult)
            ins.then_inc(scaled, 1)
            dve.wait_ge(astep, 2)
            nc.vector.reciprocal(stat[:, 3, :], stat[:, 2, :]).then_inc(vstep, 1)
            for t in range(NT):
                k = t % 2
                dve.wait_ge(turned, t + 1)
                if t >= 2:
                    dve.wait_ge(projected, t - 1)
                nc.vector.tensor_copy(hT[0:S, k, 0, :], x_ps[k][0:S, 0:P])
                nc.vector.tensor_copy(hT[0:3 * V, k, 1, :], x_ps[k][0:3 * V, P:2 * P]).then_inc(turned_sb, 1)
            dve.wait_ge(scaled, 1)

            def vecs(ap, n):
                return ap.rearrange("p j (i k) -> p j i k", i=n)

            def unit(g, a, n):
                return rhat[:, bass.ds(g * J, J), a:a + n].unsqueeze(3).broadcast_to([P, J, n, V])

            def cross_products(g, u, i):
                if not valid(g, GROUPS):
                    return
                dve.wait_ge(gathered[u], 16 * J * (i + 1))
                if valid(g - 1, GROUPS):
                    dve.wait_ge(crossed, g)
                for dst, i0, n, v0, r0 in ((0, 0, 2, 1, 2), (0, 2, 1, 0, 1), (1, 0, 1, 2, 1), (1, 1, 2, 0, 2),
                                           (2, 0, 3, 0, 0)):
                    ins = nc.vector.tensor_tensor(
                        vecs(crs[:, dst, :, i0 * V:(i0 + n) * V], n),
                        vecs(G[u][:, :, VE + v0 * V:VE + (v0 + n) * V], n),
                        unit(g, r0, n), ALU.mult)
                ins.then_inc(products, 1)

            def cross_sums(g, u):
                if not valid(g, GROUPS):
                    return
                dve.wait_ge(products, g + 1)
                nc.vector.tensor_tensor(G[u][:, :, CR:G_END], crs[:, 0], crs[:, 1], ALU.subtract)
                nc.vector.tensor_reduce(G[u][:, :, DOT:SC], crs[:, 2].rearrange("p j (i k) -> p j k i", i=3),
                                        AXX, ALU.add).then_inc(crossed, 1)

            def edge_products(g, u, c):
                dve.wait_ge(x_turned, 3 * g + c + 1)
                dve.wait_ge(w_ready, 3 * g + c + 1)
                if valid(g - 2, GROUPS):
                    dve.wait_ge(out_done, 2 * g - 2)
                nc.vector.tensor_tensor(pT[c][u % 2][:], x_ps[(3 * u + c) % 2][0:ROWS[c], :], wT[c][u % 2][:],
                                        ALU.mult).then_inc(prod_ready, 1)

            def radial_part(g, u, m):
                if not valid(g, GROUPS):
                    return
                dve.wait_ge(out_copied, 2 * g + m + 1)
                if valid(g - 1, GROUPS):
                    dve.wait_ge(msg_ready, 2 * g + m - 1)
                nc.vector.tensor_tensor(
                    radial[:, m].rearrange("p q (i k) -> p q i k", i=3),
                    msg[:, u % 2, 2 * m:2 * m + 2, Q:OUTS].unsqueeze(2).broadcast_to([P, 2, 3, V]),
                    rhat[:, bass.ds(g * J + 2 * m, 2), 2:5].unsqueeze(3).broadcast_to([P, 2, 3, V]),
                    ALU.mult).then_inc(radial_ready, 1)

            def vectors(g, u, m):
                if not valid(g, GROUPS):
                    return
                dve.wait_ge(radial_ready, 2 * g + m + 1)
                vm = msg[:, u % 2, 2 * m:2 * m + 2, SO:M]
                nc.vector.tensor_tensor(vm, vm, radial[:, m], ALU.add).then_inc(msg_ready, 1)

            def same_nodes(g, u, i):
                par, h, k = u // 2, u % 2, u % 2
                dve.wait_ge(edges_in[par], 48 * (i + 1))
                if valid(g - 2, GROUPS):
                    dve.wait_ge(summed, 2 * g - 2)
                    dve.wait_ge(idx_ready, g - 1)
                for j in range(J):
                    row = from_row[:, par, (h * J + j) * P:(h * J + j + 1) * P]
                    col = from_col[:, par, h * J + j:h * J + j + 1]
                    nc.vector.tensor_scalar(same[:, k, j, :], row, col, None, ALU.is_equal)
                    nc.vector.scalar_tensor_tensor(before[:, k, j, :], row, col, lower, ALU.is_equal, ALU.mult,
                                                   accum_out=key[:, 0, k, j:j + 1])
                nc.vector.tensor_scalar(key[:, 1, k, :], from_col[:, par, h * J:(h + 1) * J], -1.0,
                                        w[:, W_DUMP:W_DUMP + 1], ALU.mult, ALU.add).then_inc(same_ready, 1)

            def add_rows(g, u):
                k = u % 2
                dve.wait_ge(same_ready, g + 1)
                nc.vector.scalar_tensor_tensor(key[:, 2, k, :], key[:, 0, k, :], 0.5, key[:, 1, k, :],
                                               ALU.is_gt, ALU.mult).then_inc(repeats_ready, 1)

            def add_rows2(g, u):
                par, h, k = u // 2, u % 2, u % 2
                dve.wait_ge(repeats_ready, g + 1)
                if valid(g - UNROLL, GROUPS):
                    dve.wait_ge(added, 16 * J * (g - UNROLL + 1))
                nc.vector.tensor_tensor(add_idx[:, u, :], key[:, 2, k, :], from_col[:, par, h * J:(h + 1) * J],
                                        ALU.add).then_inc(idx_ready, 1)

            def step(i, u):
                g = UNROLL * i + u
                v = (u - 1) % UNROLL
                nx, ni = (u + 1) % UNROLL, i + (u + 1) // UNROLL
                cross_products(g + 1, nx, ni)
                edge_products(g, u, 0)
                radial_part(g - 1, v, 0)
                cross_sums(g + 1, nx)
                edge_products(g, u, 1)
                vectors(g - 1, v, 0)
                radial_part(g - 1, v, 1)
                same_nodes(g, u, i)
                edge_products(g, u, 2)
                add_rows(g, u)
                vectors(g - 1, v, 1)
                add_rows2(g, u)

            cross_products(0, 0, 0)
            cross_sums(0, 0)
            for u in range(UNROLL):
                step(0, u)
            with dve.Fori(1, GROUPS // UNROLL - 1) as i:
                for u in range(UNROLL):
                    step(i, u)
            for u in range(UNROLL):
                step(GROUPS // UNROLL - 1, u)
            radial_part(GROUPS - 1, 3, 0)
            radial_part(GROUPS - 1, 3, 1)
            vectors(GROUPS - 1, 3, 0)
            vectors(GROUPS - 1, 3, 1)

            n0 = 6
            for c in range(NT // CH):
                tt = slice(c * CH, (c + 1) * CH)
                pc = part[c % 2]
                dve.wait_ge(parts_in[c % 2], 16 * J * (c // 2 + 1))
                nc.vector.tensor_tensor(pc[:, 0:2], pc[:, 0:2], pc[:, 2:4], ALU.add).then_inc(keys, 1)
                dve.wait_ge(keys, n0 + 1)
                nc.vector.tensor_tensor(pc[:, 0], pc[:, 0], pc[:, 1], ALU.add).then_inc(keys, 1)
                dve.wait_ge(keys, n0 + 2)
                sca, vm, gates = nodes[:, tt, 0:SO], nodes[:, tt, NV:NALL], zeros[:, tt, :]
                nc.vector.tensor_tensor(vm, vm, pc[:, 0, :, SO:M], ALU.add)
                nc.vector.tensor_tensor(sca, sca, pc[:, 0, :, 0:SO], ALU.add).then_inc(total_ready, 1)
                dve.wait_ge(gate_ready, c + 1)
                nc.vector.tensor_tensor(sca[:, :, 0:S], sca[:, :, 0:S], gates[:, :, 0:S], ALU.mult)
                vm_i = vm.rearrange("p t (i k) -> p t i k", i=3)
                nc.vector.tensor_tensor(vm_i, vm_i, gates[:, :, S:SO].unsqueeze(2).broadcast_to([P, CH, 3, V]),
                                        ALU.mult).then_inc(keys, 1)
                dve.wait_ge(keys, n0 + 3)
                n0 += 3
                nc.vector.tensor_tensor(x_sb[:, tt, 0:S], x_sb[:, tt, 0:S], sca[:, :, 0:S], ALU.add)
                xv = x_sb[:, tt, S:F].rearrange("p t (k i) -> p t i k", i=3)
                nc.vector.tensor_tensor(xv[:, :, 0:2], xv[:, :, 0:2], vm_i[:, :, 1:3], ALU.add)
                nc.vector.tensor_tensor(xv[:, :, 2], xv[:, :, 2], vm_i[:, :, 0], ALU.add).then_inc(out_ready, 1)


def pack_weights(skip0, skip1, nl0, nl1, fc1, fc2, out_s, out_v):
    w = np.zeros((P, W_END), np.float32)

    def put(r, c, a):
        w[r:r + a.shape[0], c:c + a.shape[1]] = a

    for h in range(2):
        put(FE * h, W_FC1 + FE * h, fc1)
        c = W_FC2
        w0, w1, w2, w3, w4 = fc2[:, 0:64], fc2[:, 64:128], fc2[:, 128:160], fc2[:, 160:192], fc2[:, 192:224]
        for a in (w3, w0, w1, w2, w2, w2, w4, w4, w4):
            put(FE * h, c, a)
            c += a.shape[1]
    put(0, W_MA, out_s[S:])
    put(V, W_MA, out_s[:S])
    put(0, W_MB + 2 * V, out_v[0:S])
    put(S, W_MB, out_v[S:S + V])
    put(S + V, W_MB + V, out_v[S:S + V])
    put(0, W_MC, out_v[S:S + V])
    for i in range(3):
        put(V + i * V, W_MC + (i + 1) % 3 * V, out_v[S + V:])
        w[i:3 * V:3, W_NV + i * V:W_NV + (i + 1) * V] = nl1
        w[i:3 * V:3, W_NV + (3 + (i + 1) % 3) * V:W_NV + (4 + (i + 1) % 3) * V] = skip1
    put(0, W_NS, skip0)
    put(0, W_NS + SO, nl0)
    put(0, W_ID, np.eye(P, dtype=np.float32))
    put(0, W_LT, np.tril(np.ones((P, P), np.float32), -1))
    w[:, W_DUMP] = NPAD + np.arange(P)
    return w


def kernel(x, src, dst, edge_attr_3, edge_attr_64, L0_gnn_W_skip0, L0_gnn_W_skip1, L0_gnn_W_nl0, L0_gnn_W_nl1,
           L0_gnn_W_fc1, L0_gnn_W_fc2, L0_gnn_W_out_s, L0_gnn_W_out_v):
    import concourse.bacc as bacc
    from concourse.bass_utils import run_bass_kernel_spmd

    def padded(a, n, fill=0):
        a = np.asarray(a)
        rest = np.full((n - a.shape[0],) + a.shape[1:], fill, a.dtype)
        return np.concatenate([a, rest])

    def in_blocks(a):
        tiles = padded(a, TILES * P, 1 if a.ndim == 2 else 0).reshape(2, BLOCKS, J, P, -1)
        return np.ascontiguousarray(tiles.transpose(1, 0, 2, 3, 4)).reshape(TILES, P, -1)

    src, dst = np.asarray(src), np.asarray(dst)
    ea = np.asarray(edge_attr_3)
    ef = padded(edge_attr_64, TILES * P).reshape(2, HALF * P, FE).transpose(0, 2, 1).reshape(2 * FE, HALF * P)
    arrays = {
        "x": padded(x, NPAD),
        "wpack": pack_weights(*(np.asarray(a) for a in (
            L0_gnn_W_skip0, L0_gnn_W_skip1, L0_gnn_W_nl0, L0_gnn_W_nl1, L0_gnn_W_fc1, L0_gnn_W_fc2,
            L0_gnn_W_out_s, L0_gnn_W_out_v))),
        "edge_t": np.ascontiguousarray(ef),
        "nodes_to": np.ascontiguousarray(in_blocks(dst)[:, :, 0].T),
        "nodes_from": np.ascontiguousarray(in_blocks(src)[:, :, 0].T),
        "nodes_row": np.ascontiguousarray(in_blocks(src).reshape(1, TILES * P)),
        "edge_vec": np.ascontiguousarray(in_blocks(ea).transpose(1, 0, 2)),
    }
    nc = bacc.Bacc("TRN2", target_bir_lowering=False, num_devices=1)
    aps = {n: nc.dram_tensor(n, a.shape, mybir.dt.from_np(a.dtype), kind="ExternalInput").ap()
           for n, a in arrays.items()}
    out = nc.dram_tensor("out", (NPAD, F), F32, kind="ExternalOutput").ap()
    build_program(nc, out=out, **aps)
    r = run_bass_kernel_spmd(nc, [arrays], core_ids=[0])
    return r.results[0]["out"][:N]
```

```python
from contextlib import ExitStack

import numpy as np

import concourse.bass as bass
from concourse import mybir

ALU = mybir.AluOpType
ACT = mybir.ActivationFunctionType
AXX = mybir.AxisListType.X
F32 = mybir.dt.float32
I32 = mybir.dt.int32

P = 128
N = 3125
E = 53125
S, V = 64, 32
F = S + 3 * V
FE = 64
NT = -(-N // P)
NPAD = NT * P
TILES = 416
HALF = TILES // 2
J = 4
GROUPS = TILES // J
BLOCKS = GROUPS // 2
UNROLL = 4
GE = J * P
SO = S + V
M = SO + 3 * V
TABLE_ROWS = NPAD + P
DOT, SC, VE, CR, G_END = 0, V, V + S, V + S + 3 * V, V + S + 6 * V
E_W1, E_V, E_END = V + S, V + 2 * S, V + 2 * S + 6 * V
CHUNKS = ((0, E_W1), (E_W1, E_V + 2 * V), (E_V + 2 * V, E_END))
ROWS = tuple(b - a for a, b in CHUNKS)
Q = M
OUTS = M + V
NR = SO
NV = SO + F
NALL = NV + 3 * V
CH = 5
EPS = 1e-5

W_FC1 = 0
W_FC2 = W_FC1 + P
W_MA = W_FC2 + 2 * S + 3 * V
W_MB = W_MA + SO
W_MC = W_MB + 3 * V
W_NS = W_MC + 3 * V
W_NV = W_NS + SO + S
W_ID = W_NV + 6 * V
W_LT = W_ID + P
W_DUMP = W_LT + P
W_END = W_DUMP + 1
NFC2 = 2 * S + 3 * V
STEPS = NT // CH
PEEL = 2
TAIL = 4


def valid(k, n):
    return not isinstance(k, int) or 0 <= k < n


def build_program(nc, x, wpack, edge_t, nodes_to, nodes_from, nodes_row, edge_vec, out):
    table = nc.dram_tensor("node_table", [NPAD, F], F32, kind="Internal").ap()
    sums = [nc.dram_tensor(f"sums_{j}", [TABLE_ROWS, M], F32, kind="Internal").ap() for j in range(J)]

    with ExitStack() as ctx:
        def sb(name, shape, dt=F32):
            return ctx.enter_context(nc.sbuf_tensor(name, shape, dt))

        def ps(name, shape):
            return ctx.enter_context(nc.psum_tensor(name, shape, F32))

        def sem(name):
            return ctx.enter_context(nc.semaphore(name))

        w = sb("w", [P, W_END])
        ident = w[:, W_ID:W_ID + P]
        lower = w[:, W_LT:W_LT + P]
        x_sb = sb("x_sb", [P, NT, F])
        h_sb = sb("h_sb", [P, NT, F])
        nodes = sb("nodes", [P, NT, NALL])
        bn = sb("bn", [P, NT, 6])
        mean_var = sb("mean_var", [P, NT, 2])
        node_std = sb("node_std", [P, 5, NT])
        eps = sb("eps", [P, 1])
        hT = sb("hT", [P, 3, 2, P])
        zeros = sb("zeros", [P, TABLE_ROWS // P, M])
        rhat = sb("rhat", [P, TILES, 5])
        vec = sb("vec", [P, TILES, 3])
        vlen = sb("vlen", [P, 5, TILES])

        ef = sb("ef", [P, 2, GE])
        to_idx = sb("to_idx", [P, 2, 2 * J], I32)
        from_col = sb("from_col", [P, 2, 2 * J], I32)
        from_row = sb("from_row", [P, 2, 2 * GE], I32)
        hid = sb("hid", [P, 2, GE])
        rows = sb("rows", [P, UNROLL, J, G_END])
        crs = sb("crs", [P, 3, J, 3 * V])
        prod = sb("prod", [P, 2, J, E_END])
        pT = [[sb(f"pT{c}{k}", [ROWS[c], GE]) for k in range(2)] for c in range(3)]
        msg = sb("msg", [P, 2, J, OUTS])
        radial = sb("radial", [P, 2, 2, 3 * V])
        same = sb("same", [P, 2, J, P])
        before = sb("before", [P, 2, J, P])
        key = sb("key", [P, 3, 2, J])
        to_add = sb("to_add", [P, UNROLL, J, M])
        add_idx = sb("add_idx", [P, UNROLL, J], I32)

        hid_ps = ps("hid_ps", [P, GE])
        w_ps = [ps(f"w_ps{k}", [P, GE]) for k in range(2)]
        t_ps = [ps(f"t_ps{k}", [P, GE]) for k in range(2)]
        o_ps = [ps(f"o_ps{k}", [P, GE]) for k in range(2)]
        d_ps = ps("d_ps", [P, GE])

        w_in, vec_in = sem("w_in"), sem("vec_in")
        x_in = [sem(f"x_in{c}") for c in range(STEPS)]
        zero_set, zeroed, scaled = sem("zero_set"), sem("zeroed"), sem("scaled")
        stats_ready, std_ready, rstd_ready, normed = (
            sem(n) for n in ("stats_ready", "std_ready", "rstd_ready", "normed"))
        small = sem("small")
        turned, turned_sb, projected, nodes_ready, table_out = (
            sem(n) for n in ("turned", "turned_sb", "projected", "nodes_ready", "table_out"))
        sq_ready, len_ready, inv_ready, rhat_ready = (
            sem(n) for n in ("sq_ready", "len_ready", "inv_ready", "rhat_ready"))
        features_in = [sem(f"features_in{k}") for k in range(2)]
        from_in = [sem(f"from_in{k}") for k in range(2)]
        to_in = [sem(f"to_in{k}") for k in range(2)]
        gathered = [sem(f"gathered{u}") for u in range(UNROLL)]
        products, crossed = sem("products"), sem("crossed")
        fc1_done, hid_ready, fc2_done, prod_ready = (
            sem(n) for n in ("fc1_done", "hid_ready", "fc2_done", "prod_ready"))
        prod_turned, pT_ready = sem("prod_turned"), sem("pT_ready")
        out_done, out_copied, radial_ready, msg_ready = (
            sem(n) for n in ("out_done", "out_copied", "radial_ready", "msg_ready"))
        same_ready, repeats_ready, idx_ready = sem("same_ready"), sem("repeats_ready"), sem("idx_ready")
        summed, sums_ready, passed = sem("summed"), sem("sums_ready"), sem("passed")
        added = [sem(f"added{j}") for j in range(J)]
        parts_in = [sem(f"parts_in{k}") for k in range(2)]
        half_sum, pair_sum, total_ready, gate_ready, gated, out_ready, stored = (
            sem(n) for n in ("half_sum", "pair_sum", "total_ready", "gate_ready", "gated", "out_ready", "stored"))

        x_d = x.rearrange("(p t) f -> p t f", t=NT)
        out_d = out.rearrange("(p t) f -> p t f", t=NT)
        table_d = table.rearrange("(p t) f -> p t f", t=NT)
        sums_d = [s[0:NPAD, :].rearrange("(p t) m -> p t m", t=NT) for s in sums]
        part = [flat[:, 0:J * CH * M].rearrange("p (j t m) -> p j t m", j=J, t=CH)
                for flat in (h_sb[:, :, :].rearrange("p a b -> p (a b)"),
                             rows[:, :, :, :].rearrange("p u j f -> p (u j f)"))]
        gates = zeros[:, 0:NT, 0:SO]

        def step_of(c):
            return slice(c * CH, (c + 1) * CH)

        block = ctx.enter_context(nc.Block())

        @block.sync
        def _(sp):
            for c in range(STEPS):
                sp.dma_start(x_sb[:, step_of(c), :], x_d[:, step_of(c), :]).then_inc(x_in[c], 16)
                if c == 0:
                    sp.dma_start(w[:], wpack).then_inc(w_in, 16)
                    sp.dma_start(vec[:], edge_vec).then_inc(vec_in, 16)

            def load_to(b, par, i):
                if valid(b - 2, BLOCKS):
                    sp.wait_ge(gathered[2 * par + 1], 16 * J * i)
                sp.dma_start(to_idx[:, par, :], nodes_to[:, bass.ds(b * 2 * J, 2 * J)]).then_inc(to_in[par], 16)

            def load_features(b, par):
                if valid(b - 2, BLOCKS):
                    sp.wait_ge(fc1_done, b - 1)
                sp.dma_start(ef[:, par, :], edge_t[:, bass.ds(b * GE, GE)]).then_inc(features_in[par], 16)

            def load_from(b, par):
                if valid(b - 2, BLOCKS):
                    sp.wait_ge(idx_ready, 2 * b - 2)
                sp.dma_start(from_col[:, par, :], nodes_from[:, bass.ds(b * 2 * J, 2 * J)]).then_inc(from_in[par], 16)
                sp.dma_start(from_row[:, par, :],
                             nodes_row[:, bass.ds(b * 2 * GE, 2 * GE)].partition_broadcast(P)
                             ).then_inc(from_in[par], 16)

            for b in range(2):
                load_to(b, b, 0)
                load_features(b, b)
            load_from(0, 0)

            for c in range(STEPS):
                sp.wait_ge(nodes_ready, (c + 1) * CH)
                sp.dma_start(table_d[:, step_of(c), :], nodes[:, step_of(c), NR:NR + F]).then_inc(table_out, 16)
            for c in range(STEPS):
                sp.dma_start(sums_d[0][:, step_of(c), 0:SO], nodes[:, step_of(c), 0:SO]).then_inc(zeroed, 16)
                sp.dma_start(sums_d[0][:, step_of(c), SO:M], nodes[:, step_of(c), NV:NALL]).then_inc(zeroed, 16)
            sp.wait_ge(zero_set, 1)
            sp.dma_start(sums[0][NPAD:TABLE_ROWS, :], zeros[:, 0, :]).then_inc(zeroed, 16)
            for j in range(1, J):
                sp.dma_start(sums[j].rearrange("(p t) m -> p t m", p=P), zeros[:]).then_inc(zeroed, 16)

            load_to(2, 0, 1)
            load_features(2, 0)
            load_from(1, 1)
            load_to(3, 1, 1)
            load_features(3, 1)
            load_from(2, 0)
            with sp.Fori(2, BLOCKS // 2) as i:
                for par in range(2):
                    load_to(2 * i + par, par, i)
                    load_features(2 * i + par, par)
                    load_from(2 * i + par - 1, 1 - par)
            load_from(BLOCKS - 1, 1)

            for c in range(STEPS):
                if c >= 2:
                    sp.wait_ge(out_ready, c - 1)
                else:
                    pass
                for j in range(J):
                    sp.wait_ge(added[j], 16 * GROUPS)
                    sp.dma_start(part[c % 2][:, j], sums_d[j][:, step_of(c), :]).then_inc(parts_in[c % 2], 16)
                if c >= 1:
                    sp.wait_ge(out_ready, c)
                    sp.dma_start(out_d[:, step_of(c - 1), :], x_sb[:, step_of(c - 1), :]).then_inc(stored, 16)
            sp.wait_ge(out_ready, STEPS)
            sp.dma_start(out_d[:, step_of(STEPS - 1), :], x_sb[:, step_of(STEPS - 1), :]).then_inc(stored, 16)
            sp.wait_ge(stored, 16 * STEPS)

        @block.gpsimd
        def _(pool):
            nc.gpsimd.memset(zeros[:], 0.0).then_inc(zero_set, 1)
            pool.wait_ge(vec_in, 16)
            for i in range(3):
                ins = nc.gpsimd.tensor_tensor(vlen[:, 2 + i, :], vec[:, :, i], vec[:, :, i], ALU.mult)
            ins.then_inc(sq_ready, 1)
            pool.wait_ge(sq_ready, 1)
            nc.gpsimd.tensor_tensor(vlen[:, 2, :], vlen[:, 2, :], vlen[:, 3, :], ALU.add).then_inc(sq_ready, 1)
            pool.wait_ge(sq_ready, 2)
            nc.gpsimd.tensor_tensor(vlen[:, 0, :], vlen[:, 2, :], vlen[:, 4, :], ALU.add).then_inc(sq_ready, 1)
            pool.wait_ge(inv_ready, 1)
            for a, n in ((0, 3), (3, 2)):
                ins = nc.gpsimd.tensor_tensor(rhat[:, :, a:a + n], vec[:, :, 0:n],
                                              vlen[:, 1, :].unsqueeze(2).broadcast_to([P, TILES, n]), ALU.mult)
            ins.then_inc(rhat_ready, 1)

            def tick():
                pool.sem_inc(passed, 1)

            def gather(g, u, j, i):
                if not valid(g, GROUPS):
                    return
                par, h = u // 2, u % 2
                if j == 0:
                    if h == 0:
                        pool.wait_ge(to_in[par], 16 * (i + 1))
                    if valid(g - UNROLL, GROUPS):
                        pool.wait_ge(prod_ready, 2 * (g - UNROLL) + 2)
                        tick()
                    else:
                        pool.wait_ge(table_out, 16 * STEPS)
                pool.indirect_dma_start(
                    rows[:, u, j, SC:CR], None, table,
                    bass.IndirectOffsetOnAxis(ap=to_idx[:, par, h * J + j:h * J + j + 1], axis=0),
                ).then_inc(gathered[u], 16)

            def scatter(g, u, j):
                if not valid(g, GROUPS):
                    return
                if j == 0:
                    pool.wait_ge(idx_ready, g + 1)
                if j % 2 == 0:
                    pool.wait_ge(sums_ready, 2 * g + 1 + j // 2)
                if valid(g - 1, GROUPS):
                    pool.wait_ge(added[j], 16 * g)
                    tick()
                else:
                    pool.wait_ge(zeroed, 16 * (2 * STEPS + J))
                pool.indirect_dma_start(
                    sums[j], bass.IndirectOffsetOnAxis(ap=add_idx[:, u, j:j + 1], axis=0),
                    to_add[:, u, j, :], None, compute_op=ALU.add,
                ).then_inc(added[j], 16)

            def steps(i):
                for u in range(UNROLL):
                    g = UNROLL * i + u
                    for j in range(J):
                        gather(g + 2, (u + 2) % UNROLL, j, i + (u + 2) // UNROLL)
                        scatter(g - 4, u, j)

            for u in range(2):
                for j in range(J):
                    gather(u, u, j, 0)
            for i in range(PEEL):
                steps(i)
            with pool.Fori(PEEL, GROUPS // UNROLL - 1) as i:
                steps(i)
            steps(GROUPS // UNROLL - 1)
            for u in range(UNROLL):
                for j in range(J):
                    scatter(GROUPS - 4 + u, u, j)

            def halves(c):
                pc = part[c % 2]
                pool.wait_ge(parts_in[c % 2], 16 * J * (c // 2 + 1))
                nc.gpsimd.tensor_tensor(pc[:, 2], pc[:, 2], pc[:, 3], ALU.add).then_inc(half_sum, 1)

            def residual(c):
                pc = part[c % 2]
                pool.wait_ge(gated, c + 1)
                xt = x_sb[:, step_of(c), :]
                nc.gpsimd.tensor_tensor(xt[:, :, 0:S], xt[:, :, 0:S], pc[:, 0, :, 0:S], ALU.add)
                xv = xt[:, :, S:F].rearrange("p t (k i) -> p t i k", i=3)
                vm = pc[:, 0, :, SO:M].rearrange("p t (i k) -> p t i k", i=3)
                nc.gpsimd.tensor_tensor(xv[:, :, 0:2], xv[:, :, 0:2], vm[:, :, 1:3], ALU.add)
                nc.gpsimd.tensor_tensor(xv[:, :, 2], xv[:, :, 2], vm[:, :, 0], ALU.add).then_inc(out_ready, 1)

            for c in range(STEPS):
                halves(c)
                if c >= 1:
                    residual(c - 1)
            residual(STEPS - 1)

        @block.tensor
        def _(pe):
            pe.wait_ge(w_in, 16)

            def turn_node(t):
                if t % CH == 0:
                    pe.wait_ge(normed, t // CH + 1)
                if t >= 2:
                    pe.wait_ge(turned_sb, t - 1)
                nc.tensor.transpose(t_ps[t % 2][0:3 * V, 0:P], h_sb[:, t, 0:3 * V], ident)
                nc.tensor.transpose(t_ps[t % 2][0:3 * V, P:2 * P], h_sb[:, t, S:F], ident).then_inc(turned, 1)

            def project_node(t):
                op = (o_ps + w_ps)[t % 4]
                pe.wait_ge(turned_sb, t + 1)
                if t >= 4:
                    pe.wait_ge(nodes_ready, t - 3)
                nc.tensor.matmul(op[:, 0:SO + S], hT[0:S, t % 3, 0, :], w[0:S, W_NS:W_NS + SO + S],
                                 start=True, stop=False, skip_group_check=True)
                nc.tensor.matmul(op[:, SO + S:NALL], hT[0:3 * V, t % 3, 1, :], w[0:3 * V, W_NV:W_NV + 6 * V],
                                 start=False, stop=True, skip_group_check=True).then_inc(projected, 1)

            turn_node(0)
            for t in range(NT):
                if t + 1 < NT:
                    turn_node(t + 1)
                project_node(t)

            def fc1(b, par, i):
                if not valid(b, BLOCKS):
                    return
                pe.wait_ge(features_in[par], 16 * (i + 1))
                if valid(b - 1, BLOCKS):
                    pe.wait_ge(hid_ready, b)
                nc.tensor.matmul(hid_ps[:], w[:, W_FC1:W_FC1 + P], ef[:, par, :],
                                 start=True, stop=True).then_inc(fc1_done, 1)

            def fc2(g, u, m, b):
                if not valid(g, GROUPS):
                    return
                par, h = u // 2, u % 2
                if m == 0:
                    if h == 0:
                        pe.wait_ge(hid_ready, b + 1)
                    if isinstance(g, int) and g == 0:
                        pe.wait_ge(nodes_ready, NT)
                if valid(g - 1, GROUPS):
                    pe.wait_ge(prod_ready, 2 * g + m - 1)
                for q in range(2):
                    cols = slice((2 * m + q) * P, (2 * m + q + 1) * P)
                    ins = nc.tensor.matmul(w_ps[m][:, q * NFC2:(q + 1) * NFC2], hid[FE * h:FE * h + FE, par, cols],
                                           w[FE * h:FE * h + FE, W_FC2:W_FC2 + NFC2], start=(q == 0), stop=(q == 1),
                                           skip_group_check=True)
                ins.then_inc(fc2_done, 1)

            def turn(g, u, c):
                if not valid(g, GROUPS):
                    return
                if c == 0:
                    pe.wait_ge(prod_ready, 2 * g + 2)
                if valid(g - 1, GROUPS) or c == 2:
                    pe.wait_ge(pT_ready, 3 * g + c - 1)
                a, e = CHUNKS[c]
                for j in range(J):
                    ins = nc.tensor.transpose(t_ps[(3 * u + c) % 2][0:ROWS[c], j * P:(j + 1) * P],
                                              prod[:, u % 2, j, a:e], ident)
                ins.then_inc(prod_turned, 1)

            def outputs(g, u, m):
                if not valid(g, GROUPS):
                    return
                if m == 0:
                    pe.wait_ge(pT_ready, 3 * g + 3)
                if valid(g - 1, GROUPS):
                    pe.wait_ge(out_copied, 2 * g + m - 1)
                for q in range(2):
                    cols = slice((2 * m + q) * P, (2 * m + q + 1) * P)
                    base = q * OUTS
                    for c, (wc, oc, n) in enumerate(((W_MA, 0, SO), (W_MB, SO + V, 3 * V), (W_MC, SO, 3 * V))):
                        ins = nc.tensor.matmul(o_ps[m][:, base + oc:base + oc + n], pT[c][u % 2][:, cols],
                                               w[0:ROWS[c], wc:wc + n], start=(q == 0 and c == 0),
                                               stop=(q == 1 and c == 2), skip_group_check=True)
                ins.then_inc(out_done, 1)

            def merge(g, u, m):
                if not valid(g, GROUPS):
                    return
                pe.wait_ge(msg_ready, 2 * g + m + 1)
                if m == 0:
                    pe.wait_ge(same_ready, g + 1)
                if valid(g - 1, GROUPS) or m == 1:
                    pe.wait_ge(sums_ready, 2 * g + m)
                for q in range(2):
                    ins = nc.tensor.matmul(d_ps[:, q * M:(q + 1) * M], same[:, u % 2, 2 * m + q, :],
                                           msg[:, u % 2, 2 * m + q, 0:M], start=(q == 0), stop=(q == 1),
                                           skip_group_check=True)
                ins.then_inc(summed, 1)

            def step(i, u):
                g = UNROLL * i + u
                u1, u2, u3 = (u - 1) % UNROLL, (u - 2) % UNROLL, (u - 3) % UNROLL
                turn(g - 1, u1, 0)
                fc2(g, u, 0, 2 * i + u // 2)
                outputs(g - 2, u2, 0)
                turn(g - 1, u1, 1)
                fc2(g, u, 1, 2 * i + u // 2)
                merge(g - 3, u3, 0)
                outputs(g - 2, u2, 1)
                turn(g - 1, u1, 2)
                if u % 2 == 1:
                    fc1(2 * i + u // 2 + 1, (u // 2 + 1) % 2, i + u // 3)
                merge(g - 3, u3, 1)

            fc1(0, 0, 0)
            for u in range(UNROLL * PEEL):
                step(u // UNROLL, u % UNROLL)
            with pe.Fori(PEEL, GROUPS // UNROLL - 1) as i:
                for u in range(UNROLL):
                    step(i, u)
            for u in range(UNROLL + TAIL - 1):
                step(GROUPS // UNROLL - 1 + u // UNROLL, u % UNROLL)

        @block.scalar
        def _(act):
            act.wait_ge(w_in, 16)

            def deviation(c):
                act.wait_ge(stats_ready, c + 1)
                nc.scalar.activation(node_std[:, 0, step_of(c)], mean_var[:, step_of(c), 1], ACT.Sqrt,
                                     bias=eps[:, 0:1]).then_inc(std_ready, 1)

            def norm(c):
                act.wait_ge(rstd_ready, c + 1)
                for t in range(c * CH, (c + 1) * CH):
                    ins = nc.scalar.activation(h_sb[:, t, :], x_sb[:, t, :], ACT.Relu, bias=node_std[:, 2, t:t + 1],
                                               scale=node_std[:, 1, t:t + 1])
                ins.then_inc(normed, 1)

            for c in range(STEPS + 2):
                if c < STEPS:
                    deviation(c)
                if c == 1:
                    act.wait_ge(sq_ready, 3)
                    nc.scalar.activation(vlen[:, 1, :], vlen[:, 0, :], ACT.Sqrt).then_inc(len_ready, 1)
                if 1 <= c <= STEPS:
                    norm(c - 1)
                if c >= 2:
                    for t in range((c - 2) * CH, (c - 1) * CH):
                        act.wait_ge(projected, t + 1)
                        nc.scalar.activation(nodes[:, t, :], (o_ps + w_ps)[t % 4][:, 0:NALL],
                                             ACT.Copy).then_inc(nodes_ready, 1)

            def hidden(b, par):
                if not valid(b, BLOCKS):
                    return
                act.wait_ge(fc1_done, b + 1)
                if valid(b - 2, BLOCKS):
                    act.wait_ge(fc2_done, 4 * b - 4)
                nc.scalar.activation(hid[:, par, :], hid_ps[:], ACT.Relu).then_inc(hid_ready, 1)

            def copy_turned(g, u, c):
                if not valid(g, GROUPS):
                    return
                act.wait_ge(prod_turned, 3 * g + c + 1)
                if valid(g - 2, GROUPS):
                    act.wait_ge(out_done, 2 * g - 2)
                nc.scalar.activation(pT[c][u % 2][:], t_ps[(3 * u + c) % 2][0:ROWS[c], :],
                                     ACT.Copy).then_inc(pT_ready, 1)

            def copy_outputs(g, u, m):
                if not valid(g, GROUPS):
                    return
                act.wait_ge(out_done, 2 * g + m + 1)
                if valid(g - 2, GROUPS):
                    act.wait_ge(summed, 2 * g + m - 3)
                nc.scalar.activation(msg[:, u % 2, 2 * m:2 * m + 2, :],
                                     o_ps[m][:, 0:2 * OUTS].rearrange("p (q o) -> p q o", q=2),
                                     ACT.Copy).then_inc(out_copied, 1)

            def collect(g, u, m):
                if not valid(g, GROUPS):
                    return
                act.wait_ge(summed, 2 * g + m + 1)
                if valid(g - UNROLL, GROUPS):
                    for j in (2 * m, 2 * m + 1):
                        act.wait_ge(added[j], 16 * (g - UNROLL + 1))
                nc.scalar.activation(to_add[:, u, 2 * m:2 * m + 2, :],
                                     d_ps[:, 0:2 * M].rearrange("p (q o) -> p q o", q=2),
                                     ACT.Copy).then_inc(sums_ready, 1)

            def step(i, u):
                g = UNROLL * i + u
                u1, u2, u3 = (u - 1) % UNROLL, (u - 2) % UNROLL, (u - 3) % UNROLL
                copy_turned(g - 1, u1, 0)
                copy_outputs(g - 2, u2, 0)
                copy_turned(g - 1, u1, 1)
                collect(g - 3, u3, 0)
                copy_outputs(g - 2, u2, 1)
                copy_turned(g - 1, u1, 2)
                if u % 2 == 1:
                    hidden(2 * i + u // 2 + 1, (u // 2 + 1) % 2)
                collect(g - 3, u3, 1)

            hidden(0, 0)
            for u in range(UNROLL * PEEL):
                step(u // UNROLL, u % UNROLL)
            with act.Fori(PEEL, GROUPS // UNROLL - 1) as i:
                for u in range(UNROLL):
                    step(i, u)
            for u in range(UNROLL + TAIL - 1):
                step(GROUPS // UNROLL - 1 + u // UNROLL, u % UNROLL)

            for c in range(STEPS):
                act.wait_ge(total_ready, c + 1)
                nc.scalar.activation(gates[:, step_of(c), :], part[c % 2][:, 0, :, 0:SO],
                                     ACT.Sigmoid).then_inc(gate_ready, 1)

        @block.vector
        def _(dve):
            nc.vector.memset(eps[:], EPS)

            def statistics(c):
                dve.wait_ge(x_in[c], 16)
                for t in range(c * CH, (c + 1) * CH):
                    ins = nc.vector.bn_stats(bn[:, t, :], x_sb[:, t, :])
                ins.then_inc(small, 1)
                dve.wait_ge(small, small_at(1))
                for t in range(c * CH, (c + 1) * CH):
                    ins = nc.vector.bn_aggr(mean_var[:, t, :], bn[:, t, :])
                ins.then_inc(stats_ready, 1)

            count = [0]

            def small_at(n):
                count[0] += n
                return count[0]

            def refined(root, square, inv, t0, add):
                nc.vector.reciprocal(inv, root).then_inc(small, 1)
                dve.wait_ge(small, small_at(1))
                nc.vector.scalar_tensor_tensor(t0, square, add, inv, ALU.add, ALU.mult).then_inc(small, 1)
                dve.wait_ge(small, small_at(1))
                nc.vector.tensor_tensor(t0, t0, inv, ALU.mult).then_inc(small, 1)
                dve.wait_ge(small, small_at(1))
                nc.vector.tensor_scalar(t0, t0, -0.5, 1.5, ALU.mult, ALU.add).then_inc(small, 1)
                dve.wait_ge(small, small_at(1))
                return nc.vector.tensor_tensor(inv, inv, t0, ALU.mult)

            def inverse(c):
                dve.wait_ge(std_ready, c + 1)
                tt = step_of(c)
                refined(node_std[:, 0, tt], mean_var[:, tt, 1], node_std[:, 1, tt], node_std[:, 3, tt],
                        EPS).then_inc(small, 1)
                dve.wait_ge(small, small_at(1))
                nc.vector.scalar_tensor_tensor(node_std[:, 2, tt], mean_var[:, tt, 0], -1.0, node_std[:, 1, tt],
                                               ALU.mult, ALU.mult).then_inc(rstd_ready, 1)

            def copy_node(t):
                dve.wait_ge(turned, t + 1)
                if t >= 3:
                    dve.wait_ge(projected, t - 2)
                nc.vector.tensor_copy(hT[0:3 * V, t % 3, :, :],
                                      t_ps[t % 2][0:3 * V, 0:2 * P].rearrange("p (a b) -> p a b", a=2)
                                      ).then_inc(turned_sb, 1)

            for c in range(STEPS + 2):
                if c < STEPS:
                    statistics(c)
                if 1 <= c <= STEPS:
                    inverse(c - 1)
                if c >= 2:
                    for t in range((c - 2) * CH, (c - 1) * CH):
                        copy_node(t)
                if c == 2:
                    dve.wait_ge(len_ready, 1)
                    nc.vector.tensor_copy(vlen[:, 3, :], vlen[:, 1, :]).then_inc(small, 1)
                    dve.wait_ge(small, small_at(1))
                    refined(vlen[:, 3, :], vlen[:, 0, :], vlen[:, 1, :], vlen[:, 2, :], 0.0).then_inc(inv_ready, 1)

            dve.wait_ge(w_in, 16)
            for r0 in range(0, P, V):
                for wc, n, scale in ((W_MA, SO, 1.0), (W_MB, 3 * V, 3 ** 0.5 if r0 < S else 1.0),
                                     (W_MC, 3 * V, 1.0 if r0 < V else 1.5 ** 0.5)):
                    if wc == W_MA and r0 >= SO:
                        continue
                    ins = nc.vector.tensor_scalar(w[r0:r0 + V, wc:wc + n], w[r0:r0 + V, wc:wc + n],
                                                  scale / 32.0, None, ALU.mult)
            ins.then_inc(scaled, 1)
            dve.wait_ge(scaled, 1)
            dve.wait_ge(rhat_ready, 1)

            def vecs(ap, n):
                return ap.rearrange("p j (i k) -> p j i k", i=n)

            def unit(g, a, n):
                return rhat[:, bass.ds(g * J, J), a:a + n].unsqueeze(3).broadcast_to([P, J, n, V])

            def cross_products(g, u, i):
                if not valid(g, GROUPS):
                    return
                dve.wait_ge(gathered[u], 16 * J * (i + 1))
                if valid(g - 1, GROUPS):
                    dve.wait_ge(crossed, g)
                for dst, i0, n, v0, r0 in ((0, 0, 2, 1, 2), (0, 2, 1, 0, 1), (1, 0, 1, 2, 1), (1, 1, 2, 0, 2),
                                           (2, 0, 3, 0, 0)):
                    ins = nc.vector.tensor_tensor(
                        vecs(crs[:, dst, :, i0 * V:(i0 + n) * V], n),
                        vecs(rows[:, u, :, VE + v0 * V:VE + (v0 + n) * V], n),
                        unit(g, r0, n), ALU.mult)
                ins.then_inc(products, 1)

            def cross_sums(g, u):
                if not valid(g, GROUPS):
                    return
                dve.wait_ge(products, g + 1)
                nc.vector.tensor_tensor(rows[:, u, :, CR:G_END], crs[:, 0], crs[:, 1], ALU.subtract)
                nc.vector.tensor_reduce(rows[:, u, :, DOT:SC], crs[:, 2].rearrange("p j (i k) -> p j k i", i=3),
                                        AXX, ALU.add).then_inc(crossed, 1)

            def edge_products(g, u, m):
                if not valid(g, GROUPS):
                    return
                dve.wait_ge(fc2_done, 2 * g + m + 1)
                if m == 0:
                    dve.wait_ge(crossed, g + 1)
                    if valid(g - 2, GROUPS):
                        dve.wait_ge(prod_turned, 3 * g - 3)
                jj = slice(2 * m, 2 * m + 2)
                we = w_ps[m][:, 0:2 * NFC2].rearrange("p (q n) -> p q n", q=2)
                gr, pr = rows[:, u, jj], prod[:, u % 2, jj]
                nc.vector.tensor_tensor(pr[:, :, 0:E_W1], we[:, :, 0:E_W1], gr[:, :, DOT:VE], ALU.mult)
                nc.vector.tensor_tensor(pr[:, :, E_W1:E_V], we[:, :, E_W1:E_V], gr[:, :, SC:VE], ALU.mult)
                for n, (a, b) in enumerate(((VE, CR), (CR, G_END))):
                    ins = nc.vector.tensor_tensor(
                        vecs(pr[:, :, E_V + 3 * V * n:E_V + 3 * V * (n + 1)], 3),
                        we[:, :, E_V + V * n:E_V + V * (n + 1)].unsqueeze(2).broadcast_to([P, 2, 3, V]),
                        vecs(gr[:, :, a:b], 3), ALU.mult)
                ins.then_inc(prod_ready, 1)

            def radial_part(g, u, m):
                if not valid(g, GROUPS):
                    return
                dve.wait_ge(out_copied, 2 * g + m + 1)
                if valid(g - 1, GROUPS):
                    dve.wait_ge(msg_ready, 2 * g + m - 1)
                nc.vector.tensor_tensor(
                    radial[:, m].rearrange("p q (i k) -> p q i k", i=3),
                    msg[:, u % 2, 2 * m:2 * m + 2, Q:OUTS].unsqueeze(2).broadcast_to([P, 2, 3, V]),
                    rhat[:, bass.ds(g * J + 2 * m, 2), 2:5].unsqueeze(3).broadcast_to([P, 2, 3, V]),
                    ALU.mult).then_inc(radial_ready, 1)

            def vectors(g, u, m):
                if not valid(g, GROUPS):
                    return
                dve.wait_ge(radial_ready, 2 * g + m + 1)
                vm = msg[:, u % 2, 2 * m:2 * m + 2, SO:M]
                nc.vector.tensor_tensor(vm, vm, radial[:, m], ALU.add).then_inc(msg_ready, 1)

            def same_nodes(g, u, i):
                if not valid(g, GROUPS):
                    return
                par, h, k = u // 2, u % 2, u % 2
                dve.wait_ge(from_in[par], 32 * (i + 1))
                if valid(g - 2, GROUPS):
                    dve.wait_ge(summed, 2 * g - 2)
                    dve.wait_ge(idx_ready, g - 1)
                for j in range(J):
                    row = from_row[:, par, (h * J + j) * P:(h * J + j + 1) * P]
                    col = from_col[:, par, h * J + j:h * J + j + 1]
                    nc.vector.tensor_scalar(same[:, k, j, :], row, col, None, ALU.is_equal)
                    nc.vector.scalar_tensor_tensor(before[:, k, j, :], row, col, lower, ALU.is_equal, ALU.mult,
                                                   accum_out=key[:, 0, k, j:j + 1])
                nc.vector.tensor_scalar(key[:, 1, k, :], from_col[:, par, h * J:(h + 1) * J], -1.0,
                                        w[:, W_DUMP:W_DUMP + 1], ALU.mult, ALU.add).then_inc(same_ready, 1)

            def repeats(g, u):
                if not valid(g, GROUPS):
                    return
                k = u % 2
                dve.wait_ge(same_ready, g + 1)
                nc.vector.scalar_tensor_tensor(key[:, 2, k, :], key[:, 0, k, :], 0.5, key[:, 1, k, :],
                                               ALU.is_gt, ALU.mult).then_inc(repeats_ready, 1)

            def rows_to_add(g, u):
                if not valid(g, GROUPS):
                    return
                par, h, k = u // 2, u % 2, u % 2
                dve.wait_ge(repeats_ready, g + 1)
                if valid(g - UNROLL, GROUPS):
                    for j in range(J):
                        dve.wait_ge(added[j], 16 * (g - UNROLL + 1))
                nc.vector.tensor_tensor(add_idx[:, u, :], key[:, 2, k, :], from_col[:, par, h * J:(h + 1) * J],
                                        ALU.add).then_inc(idx_ready, 1)

            def step(i, u):
                g = UNROLL * i + u
                u2 = (u - 2) % UNROLL
                nx, ni = (u + 1) % UNROLL, i + (u + 1) // UNROLL
                cross_products(g + 1, nx, ni)
                edge_products(g, u, 0)
                radial_part(g - 2, u2, 0)
                cross_sums(g + 1, nx)
                edge_products(g, u, 1)
                vectors(g - 2, u2, 0)
                same_nodes(g - 2, u2, i - (1 if u < 2 else 0))
                radial_part(g - 2, u2, 1)
                repeats(g - 2, u2)
                vectors(g - 2, u2, 1)
                rows_to_add(g - 2, u2)

            cross_products(0, 0, 0)
            cross_sums(0, 0)
            for u in range(UNROLL * PEEL):
                step(u // UNROLL, u % UNROLL)
            with dve.Fori(PEEL, GROUPS // UNROLL - 1) as i:
                for u in range(UNROLL):
                    step(i, u)
            for u in range(UNROLL + TAIL - 2):
                step(GROUPS // UNROLL - 1 + u // UNROLL, u % UNROLL)

            def total(c):
                pc = part[c % 2]
                dve.wait_ge(parts_in[c % 2], 16 * J * (c // 2 + 1))
                nc.vector.tensor_tensor(pc[:, 0], pc[:, 0], pc[:, 1], ALU.add).then_inc(pair_sum, 1)
                dve.wait_ge(pair_sum, c + 1)
                dve.wait_ge(half_sum, c + 1)
                nc.vector.tensor_tensor(pc[:, 0], pc[:, 0], pc[:, 2], ALU.add).then_inc(total_ready, 1)

            def gate(c):
                pc, gt = part[c % 2][:, 0], gates[:, step_of(c), :]
                dve.wait_ge(gate_ready, c + 1)
                nc.vector.tensor_tensor(pc[:, :, 0:S], pc[:, :, 0:S], gt[:, :, 0:S], ALU.mult)
                vm = pc[:, :, SO:M].rearrange("p t (i k) -> p t i k", i=3)
                nc.vector.tensor_tensor(vm, vm, gt[:, :, S:SO].unsqueeze(2).broadcast_to([P, CH, 3, V]),
                                        ALU.mult).then_inc(gated, 1)

            for c in range(STEPS):
                total(c)
                if c >= 1:
                    gate(c - 1)
            gate(STEPS - 1)


def pack_weights(skip0, skip1, nl0, nl1, fc1, fc2, out_s, out_v):
    w = np.zeros((P, W_END), np.float32)

    def put(r, c, a):
        w[r:r + a.shape[0], c:c + a.shape[1]] = a

    for h in range(2):
        put(FE * h, W_FC1 + FE * h, fc1)
        c = W_FC2
        w0, w1, w2, w3, w4 = fc2[:, 0:64], fc2[:, 64:128], fc2[:, 128:160], fc2[:, 160:192], fc2[:, 192:224]
        for a in (w3, w0, w1, w2, w4):
            put(FE * h, c, a)
            c += a.shape[1]
    put(0, W_MA, out_s[S:])
    put(V, W_MA, out_s[:S])
    put(0, W_MB + 2 * V, out_v[0:S])
    put(S, W_MB, out_v[S:S + V])
    put(S + V, W_MB + V, out_v[S:S + V])
    put(0, W_MC, out_v[S:S + V])
    for i in range(3):
        put(V + i * V, W_MC + (i + 1) % 3 * V, out_v[S + V:])
        w[i:3 * V:3, W_NV + i * V:W_NV + (i + 1) * V] = nl1
        w[i:3 * V:3, W_NV + (3 + (i + 1) % 3) * V:W_NV + (4 + (i + 1) % 3) * V] = skip1
    put(0, W_NS, skip0)
    put(0, W_NS + SO, nl0)
    put(0, W_ID, np.eye(P, dtype=np.float32))
    put(0, W_LT, np.tril(np.ones((P, P), np.float32), -1))
    w[:, W_DUMP] = NPAD + np.arange(P)
    return w


def kernel(x, src, dst, edge_attr_3, edge_attr_64, L0_gnn_W_skip0, L0_gnn_W_skip1, L0_gnn_W_nl0, L0_gnn_W_nl1,
           L0_gnn_W_fc1, L0_gnn_W_fc2, L0_gnn_W_out_s, L0_gnn_W_out_v):
    import concourse.bacc as bacc
    from concourse.bass_utils import run_bass_kernel_spmd

    def padded(a, n, fill=0):
        a = np.asarray(a)
        rest = np.full((n - a.shape[0],) + a.shape[1:], fill, a.dtype)
        return np.concatenate([a, rest])

    def in_blocks(a):
        tiles = padded(a, TILES * P, 1 if a.ndim == 2 else 0).reshape(2, BLOCKS, J, P, -1)
        return np.ascontiguousarray(tiles.transpose(1, 0, 2, 3, 4)).reshape(TILES, P, -1)

    src, dst = np.asarray(src), np.asarray(dst)
    ea = np.asarray(edge_attr_3)
    ef = padded(edge_attr_64, TILES * P).reshape(2, HALF * P, FE).transpose(0, 2, 1).reshape(2 * FE, HALF * P)
    arrays = {
        "x": padded(x, NPAD),
        "wpack": pack_weights(*(np.asarray(a) for a in (
            L0_gnn_W_skip0, L0_gnn_W_skip1, L0_gnn_W_nl0, L0_gnn_W_nl1, L0_gnn_W_fc1, L0_gnn_W_fc2,
            L0_gnn_W_out_s, L0_gnn_W_out_v))),
        "edge_t": np.ascontiguousarray(ef),
        "nodes_to": np.ascontiguousarray(in_blocks(dst)[:, :, 0].T),
        "nodes_from": np.ascontiguousarray(in_blocks(src)[:, :, 0].T),
        "nodes_row": np.ascontiguousarray(in_blocks(src).reshape(1, TILES * P)),
        "edge_vec": np.ascontiguousarray(in_blocks(ea).transpose(1, 0, 2)),
    }
    nc = bacc.Bacc("TRN2", target_bir_lowering=False, num_devices=1)
    aps = {n: nc.dram_tensor(n, a.shape, mybir.dt.from_np(a.dtype), kind="ExternalInput").ap()
           for n, a in arrays.items()}
    out = nc.dram_tensor("out", (NPAD, F), F32, kind="ExternalOutput").ap()
    build_program(nc, out=out, **aps)
    r = run_bass_kernel_spmd(nc, [arrays], core_ids=[0])
    return r.results[0]["out"][:N]
```

```python
from contextlib import ExitStack

import numpy as np

import concourse.bass as bass
from concourse import mybir

ALU = mybir.AluOpType
ACT = mybir.ActivationFunctionType
AXX = mybir.AxisListType.X
F32 = mybir.dt.float32
I32 = mybir.dt.int32

P = 128
N = 3125
E = 53125
S, V = 64, 32
F = S + 3 * V
FE = 64
NT = -(-N // P)
NPAD = NT * P
TILES = 416
HALF = TILES // 2
J = 4
GROUPS = TILES // J
BLOCKS = GROUPS // 2
UNROLL = 4
GE = J * P
SO = S + V
M = SO + 3 * V
TABLE_ROWS = NPAD + P
DOT, SC, VE, CR, G_END = 0, V, V + S, V + S + 3 * V, V + S + 6 * V
E_W1, E_V, E_END = V + S, V + 2 * S, V + 2 * S + 6 * V
CHUNKS = ((0, E_W1), (E_W1, E_V + 2 * V), (E_V + 2 * V, E_END))
ROWS = tuple(b - a for a, b in CHUNKS)
Q = M
OUTS = M + V
CH = 5
EPS = 1e-5

W_FC1 = 0
W_FC2 = W_FC1 + P
W_MA = W_FC2 + 2 * S + 3 * V
W_MB = W_MA + SO
W_MC = W_MB + 3 * V
W_NS = W_MC + 3 * V
W_NV = W_NS + SO + S
W_ID = W_NV + 6 * V
W_LT = W_ID + P
W_DUMP = W_LT + P
W_END = W_DUMP + 1
NFC2 = 2 * S + 3 * V
STEPS = NT // CH
SCALES = ((0, 1), (1, 3), (3, 5))
LAST = [slice(a, min(a + n, NT)) for a, n in ((0, 5), (5, 5), (10, 5), (15, 5), (20, 3), (23, 2))]
SKIP_PAIRS = -(-NT // 2)
ZR = 7
ZERO_RUNS = [(a, min(a + ZR, TABLE_ROWS // P)) for a in range(0, TABLE_ROWS // P, ZR)]
ZERO_PARTS = [(j, a, e) for a, e in ZERO_RUNS for j in range(J)]
EARLY_ZEROS = 4
EARLY_GROUPS = 2
LEAD, LAG = 3, 4
WARM_UP = 2
PEEL = 2
TAIL = 4


def valid(k, n):
    return not isinstance(k, int) or 0 <= k < n


def build_program(nc, x, wpack, edge_t, nodes_to, nodes_from, nodes_row, edge_vec, out):
    table = nc.dram_tensor("node_table", [NPAD, F], F32, kind="Internal").ap()
    sums = [nc.dram_tensor(f"sums_{j}", [TABLE_ROWS, M], F32, kind="Internal").ap() for j in range(J)]

    with ExitStack() as ctx:
        def sb(name, shape, dt=F32):
            return ctx.enter_context(nc.sbuf_tensor(name, shape, dt))

        def ps(name, shape):
            return ctx.enter_context(nc.psum_tensor(name, shape, F32))

        def sem(name):
            return ctx.enter_context(nc.semaphore(name))

        w = sb("w", [P, W_END])
        ident = w[:, W_ID:W_ID + P]
        lower = w[:, W_LT:W_LT + P]
        x_sb = sb("x_sb", [P, NT, F])
        h_sb = sb("h_sb", [P, NT, F])
        node_rows = sb("node_rows", [P, NT, F])
        skip = sb("skip", [P, NT, M])
        bn = sb("bn", [P, NT, 6])
        mean_var = sb("mean_var", [P, NT, 2])
        node_std = sb("node_std", [P, 5, NT])
        eps = sb("eps", [P, 2])
        hT = sb("hT", [P, NT, 2, P])
        zeros = sb("zeros", [P, ZR, M])
        rhat = sb("rhat", [P, TILES, 5])

        ef = sb("ef", [P, 2, GE])
        to_idx = sb("to_idx", [P, 2, 2 * J], I32)
        from_col = sb("from_col", [P, 2, 2 * J], I32)
        from_row = sb("from_row", [P, 2, 2 * GE], I32)
        hid = sb("hid", [P, 2, GE])
        rows = sb("rows", [P, UNROLL, J, G_END])
        products_space = sb("products_space", [P, 3 * J * 3 * V + 2 * J * E_END])
        crs = products_space[:, 0:3 * J * 3 * V].rearrange("p (n j f) -> p n j f", n=3, j=J)
        prod = products_space[:, 3 * J * 3 * V:].rearrange("p (k j f) -> p k j f", k=2, j=J)
        pT = [[sb(f"pT{c}{k}", [ROWS[c], GE]) for k in range(2)] for c in range(3)]
        msg = sb("msg", [P, 2, J, OUTS])
        radial = sb("radial", [P, 2, 2, 3 * V])
        same = sb("same", [P, 2, J, P])
        before = sb("before", [P, 2, J, P])
        key = sb("key", [P, 3, 2, J])
        to_add = sb("to_add", [P, UNROLL, J, M])
        add_idx = sb("add_idx", [P, UNROLL, J], I32)

        vec = msg[:, :, :, :].rearrange("p k j f -> p (k j f)")[:, 0:3 * TILES].rearrange("p (t i) -> p t i", i=3)
        vlen = to_add[:, :, :, :].rearrange("p u j m -> p (u j m)")[:, 0:5 * TILES].rearrange("p (k t) -> p k t", k=5)

        hid_ps = ps("hid_ps", [P, GE])
        w_ps = [ps(f"w_ps{k}", [P, GE]) for k in range(2)]
        t_ps = [ps(f"t_ps{k}", [P, GE]) for k in range(2)]
        o_ps = [ps(f"o_ps{k}", [P, GE]) for k in range(2)]
        d_ps = ps("d_ps", [P, GE])

        w_in, vec_in = sem("w_in"), sem("vec_in")
        x_in = [sem(f"x_in{c}") for c in range(STEPS)]
        zero_set, zeroed, scaled = sem("zero_set"), sem("zeroed"), sem("scaled")
        eps_set, stats_ready, std_ready, rstd_ready, centered = (
            sem(n) for n in ("eps_set", "stats_ready", "std_ready", "rstd_ready", "centered"))
        small = sem("small")
        turned, turned_sb, projected, rows_ready, skip_ready, table_out = (
            sem(n) for n in ("turned", "turned_sb", "projected", "rows_ready", "skip_ready", "table_out"))
        sq_ready, len_ready, rhat_ready = (
            sem(n) for n in ("sq_ready", "len_ready", "rhat_ready"))
        features_in = [sem(f"features_in{k}") for k in range(2)]
        from_in = [sem(f"from_in{k}") for k in range(2)]
        to_in = [sem(f"to_in{k}") for k in range(2)]
        gathered = [sem(f"gathered{u}") for u in range(UNROLL)]
        products, crossed = sem("products"), sem("crossed")
        fc1_done, hid_ready, fc2_done, prod_ready = (
            sem(n) for n in ("fc1_done", "hid_ready", "fc2_done", "prod_ready"))
        prod_turned, pT_ready = sem("prod_turned"), sem("pT_ready")
        out_done, out_copied, radial_ready, msg_ready = (
            sem(n) for n in ("out_done", "out_copied", "radial_ready", "msg_ready"))
        same_ready, repeats_ready, idx_ready = sem("same_ready"), sem("repeats_ready"), sem("idx_ready")
        summed, sums_ready, passed = sem("summed"), sem("sums_ready"), sem("passed")
        added = [sem(f"added{j}") for j in range(J)]
        three_in = [sem(f"three_in{c}") for c in range(len(LAST))]
        fourth_in = [sem(f"fourth_in{c}") for c in range(len(LAST))]
        skip_done, with_skip = sem("skip_done"), sem("with_skip")
        half_sum, pair_sum, total_ready, gate_ready, gated, out_ready, stored = (
            sem(n) for n in ("half_sum", "pair_sum", "total_ready", "gate_ready", "gated", "out_ready", "stored"))

        x_d = x.rearrange("(p t) f -> p t f", t=NT)
        out_d = out.rearrange("(p t) f -> p t f", t=NT)
        table_d = table.rearrange("(p t) f -> p t f", t=NT)
        sums_d = [s[0:NPAD, :].rearrange("(p t) m -> p t m", t=NT) for s in sums]
        part = [flat[:, 0:J * CH * M].rearrange("p (j t m) -> p j t m", j=J, t=CH)
                for flat in (h_sb[:, :, :].rearrange("p a b -> p (a b)"),
                             rows[:, :, :, :].rearrange("p u j f -> p (u j f)"),
                             node_rows[:, :, :].rearrange("p t f -> p (t f)"),
                             hT[:, :, :, :].rearrange("p t a b -> p (t a b)"),
                             products_space[:, :])]
        part.append(part[0])
        gates = to_add[:, :, :, :].rearrange("p u j m -> p (u j m)")[:, 0:NT * SO].rearrange("p (t s) -> p t s", s=SO)

        def step_of(c):
            return slice(c * CH, (c + 1) * CH)

        def set_zero(engine, j, a, e):
            engine.dma_start(sums[j].rearrange("(p t) m -> p t m", p=P)[:, a:e, :],
                             zeros[:, 0:e - a, :]).then_inc(zeroed, 16)

        block = ctx.enter_context(nc.Block())

        @block.sync
        def _(sp):
            for c in range(STEPS):
                sp.dma_start(x_sb[:, step_of(c), :], x_d[:, step_of(c), :]).then_inc(x_in[c], 16)
                if c == 0:
                    sp.dma_start(w[:], wpack).then_inc(w_in, 16)
                if c == 1:
                    sp.dma_start(vec, edge_vec).then_inc(vec_in, 16)

            def load_to(b, par, i):
                if valid(b - 2, BLOCKS):
                    sp.wait_ge(gathered[2 * par + 1], 16 * J * i)
                sp.dma_start(to_idx[:, par, :], nodes_to[:, bass.ds(b * 2 * J, 2 * J)]).then_inc(to_in[par], 16)

            def load_features(b, par):
                if valid(b - 2, BLOCKS):
                    sp.wait_ge(fc1_done, b - 1)
                sp.dma_start(ef[:, par, :], edge_t[:, bass.ds(b * GE, GE)]).then_inc(features_in[par], 16)

            def load_from(b, par):
                if valid(b - 2, BLOCKS):
                    sp.wait_ge(idx_ready, 2 * b - 2)
                sp.dma_start(from_col[:, par, :], nodes_from[:, bass.ds(b * 2 * J, 2 * J)]).then_inc(from_in[par], 16)
                sp.dma_start(from_row[:, par, :],
                             nodes_row[:, bass.ds(b * 2 * GE, 2 * GE)].partition_broadcast(P)
                             ).then_inc(from_in[par], 16)

            for b in range(2):
                load_to(b, b, 0)
                load_features(b, b)
            load_from(0, 0)

            sp.wait_ge(zero_set, 1)
            for part_of_sums in ZERO_PARTS[:EARLY_ZEROS]:
                set_zero(sp, *part_of_sums)

            for c in range(STEPS):
                sp.wait_ge(rows_ready, (c + 1) * CH)
                sp.dma_start(table_d[:, step_of(c), :], node_rows[:, step_of(c), :]).then_inc(table_out, 16)
            load_to(2, 0, 1)
            load_features(2, 0)
            load_from(1, 1)
            load_to(3, 1, 1)
            load_features(3, 1)
            load_from(2, 0)
            with sp.Fori(2, BLOCKS // 2) as i:
                for par in range(2):
                    load_to(2 * i + par, par, i)
                    load_features(2 * i + par, par)
                    load_from(2 * i + par - 1, 1 - par)
            load_from(BLOCKS - 1, 1)

            def load_sums(c, tables):
                if c == 3:
                    sp.wait_ge(skip_ready, SKIP_PAIRS)
                if c == 5:
                    sp.wait_ge(out_ready, 1)
                for j in tables:
                    if c == 0:
                        sp.wait_ge(added[j], 16 * GROUPS)
                    n = LAST[c].stop - LAST[c].start
                    sp.dma_start(part[c][:, j, 0:n], sums_d[j][:, LAST[c], :]
                                 ).then_inc(fourth_in[c] if j == J - 1 else three_in[c], 16)

            for c, tables in ((0, [0]), (1, [0]), (0, [1]), (0, [2]), (1, [1, 2]), (0, [3]), (1, [3])):
                load_sums(c, tables)
            for c in range(2, len(LAST)):
                load_sums(c, range(J))
            for c, tt in enumerate(LAST):
                sp.wait_ge(out_ready, c + 1)
                sp.dma_start(out_d[:, tt, :], x_sb[:, tt, :]).then_inc(stored, 16)
            sp.wait_ge(stored, 16 * len(LAST))

        @block.gpsimd
        def _(pool):
            nc.gpsimd.memset(zeros[:], 0.0).then_inc(zero_set, 1)
            pool.wait_ge(vec_in, 16)
            for i in range(3):
                ins = nc.gpsimd.tensor_tensor(vlen[:, 2 + i, :], vec[:, :, i], vec[:, :, i], ALU.mult)
            ins.then_inc(sq_ready, 1)
            pool.wait_ge(sq_ready, 1)
            nc.gpsimd.tensor_tensor(vlen[:, 2, :], vlen[:, 2, :], vlen[:, 3, :], ALU.add).then_inc(sq_ready, 1)
            pool.wait_ge(sq_ready, 2)
            nc.gpsimd.tensor_tensor(vlen[:, 0, :], vlen[:, 2, :], vlen[:, 4, :], ALU.add).then_inc(sq_ready, 1)

            def tick():
                pool.sem_inc(passed, 1)

            def gather(g, u, j, i):
                if not valid(g, GROUPS):
                    return
                par, h = u // 2, u % 2
                if j == 0:
                    if h == 0:
                        pool.wait_ge(to_in[par], 16 * (i + 1))
                    if valid(g - UNROLL, GROUPS):
                        pool.wait_ge(prod_ready, 2 * (g - UNROLL) + 2)
                        tick()
                    else:
                        pool.wait_ge(table_out, 16 * STEPS)
                pool.indirect_dma_start(
                    rows[:, u, j, SC:CR], None, table,
                    bass.IndirectOffsetOnAxis(ap=to_idx[:, par, h * J + j:h * J + j + 1], axis=0),
                ).then_inc(gathered[u], 16)

            def scatter(g, u, j):
                if not valid(g, GROUPS):
                    return
                if j == 0:
                    pool.wait_ge(idx_ready, g + 1)
                if j % 2 == 0:
                    pool.wait_ge(sums_ready, 2 * g + 1 + j // 2)
                if valid(g - 1, GROUPS):
                    pool.wait_ge(added[j], 16 * g)
                    tick()
                else:
                    pool.wait_ge(zeroed, 16 * len(ZERO_PARTS))
                pool.indirect_dma_start(
                    sums[j], bass.IndirectOffsetOnAxis(ap=add_idx[:, u, j:j + 1], axis=0),
                    to_add[:, u, j, :], None, compute_op=ALU.add,
                ).then_inc(added[j], 16)

            def steps(i):
                for u in range(UNROLL):
                    g = UNROLL * i + u
                    for j in range(J):
                        gather(g + LEAD, (u + LEAD) % UNROLL, j, i + (u + LEAD) // UNROLL)
                        scatter(g - LAG, (u - LAG) % UNROLL, j)

            for u in range(LEAD):
                for j in range(J):
                    gather(u, u, j, 0)
            for i in range(PEEL):
                steps(i)
            with pool.Fori(PEEL, GROUPS // UNROLL - 1) as i:
                steps(i)
            steps(GROUPS // UNROLL - 1)
            for g in range(GROUPS - LAG, GROUPS):
                for j in range(J):
                    scatter(g, g % UNROLL, j)

            pool.wait_ge(skip_ready, SKIP_PAIRS)
            for c, tt in enumerate(LAST):
                pc = part[c][:, :, 0:tt.stop - tt.start]
                pool.wait_ge(three_in[c], 16 * 3)
                nc.gpsimd.tensor_tensor(pc[:, 2], pc[:, 2], skip[:, tt, :], ALU.add).then_inc(with_skip, 1)
                if c < len(LAST) - 1:
                    pool.wait_ge(with_skip, c + 1)
                    pool.wait_ge(fourth_in[c], 16)
                    nc.gpsimd.tensor_tensor(pc[:, 2], pc[:, 2], pc[:, 3], ALU.add).then_inc(half_sum, 1)

        @block.tensor
        def _(pe):
            pe.wait_ge(w_in, 16)

            for _ in range(WARM_UP):
                nc.tensor.matmul(d_ps[:], ident, w[:, 0:GE], start=True, stop=True)

            def turn_node(t):
                if t % CH == 0:
                    pe.wait_ge(centered, t // CH + 1)
                if t >= 2:
                    pe.wait_ge(turned_sb, t - 1)
                nc.tensor.transpose(t_ps[t % 2][0:3 * V, 0:P], h_sb[:, t, 0:3 * V], ident)
                nc.tensor.transpose(t_ps[t % 2][0:3 * V, P:2 * P], h_sb[:, t, S:F], ident).then_inc(turned, 1)

            def project_node(t):
                op = (o_ps + w_ps)[t % 4]
                pe.wait_ge(turned_sb, t + 1)
                if t >= 4:
                    pe.wait_ge(rows_ready, t - 3)
                nc.tensor.matmul(op[:, 0:S], hT[0:S, t, 0, :], w[0:S, W_NS + SO:W_NS + SO + S],
                                 start=True, stop=False, skip_group_check=True)
                nc.tensor.matmul(op[:, S:F], hT[0:3 * V, t, 1, :], w[0:3 * V, W_NV:W_NV + 3 * V],
                                 start=False, stop=True, skip_group_check=True).then_inc(projected, 1)

            turn_node(0)
            for t in range(NT):
                if t + 1 < NT:
                    turn_node(t + 1)
                project_node(t)

            def skip_products(n):
                bank = (d_ps, o_ps[0])[n % 2]
                pe.wait_ge(rows_ready, NT)
                if n >= 2:
                    pe.wait_ge(skip_ready, n - 1)
                tiles = range(2 * n, min(2 * n + 2, NT))
                for q, t in enumerate(tiles):
                    nc.tensor.matmul(bank[:, q * M:q * M + SO], hT[0:S, t, 0, :], w[0:S, W_NS:W_NS + SO],
                                     start=(q == 0), stop=False, skip_group_check=True)
                    ins = nc.tensor.matmul(bank[:, q * M + SO:(q + 1) * M], hT[0:3 * V, t, 1, :],
                                           w[0:3 * V, W_NV + 3 * V:W_NV + 6 * V], start=False,
                                           stop=(t == tiles[-1]), skip_group_check=True)
                ins.then_inc(skip_done, 1)

            def fc1(b, par, i):
                if not valid(b, BLOCKS):
                    return
                pe.wait_ge(features_in[par], 16 * (i + 1))
                if valid(b - 1, BLOCKS):
                    pe.wait_ge(hid_ready, b)
                nc.tensor.matmul(hid_ps[:], w[:, W_FC1:W_FC1 + P], ef[:, par, :],
                                 start=True, stop=True).then_inc(fc1_done, 1)

            def fc2(g, u, m, b):
                if not valid(g, GROUPS):
                    return
                par, h = u // 2, u % 2
                if m == 0:
                    if h == 0:
                        pe.wait_ge(hid_ready, b + 1)
                    if isinstance(g, int) and g == 0:
                        pe.wait_ge(rows_ready, NT)
                if valid(g - 1, GROUPS):
                    pe.wait_ge(prod_ready, 2 * g + m - 1)
                for q in range(2):
                    cols = slice((2 * m + q) * P, (2 * m + q + 1) * P)
                    ins = nc.tensor.matmul(w_ps[m][:, q * NFC2:(q + 1) * NFC2], hid[FE * h:FE * h + FE, par, cols],
                                           w[FE * h:FE * h + FE, W_FC2:W_FC2 + NFC2], start=(q == 0), stop=(q == 1),
                                           skip_group_check=True)
                ins.then_inc(fc2_done, 1)

            def turn(g, u, c):
                if not valid(g, GROUPS):
                    return
                if c == 0:
                    pe.wait_ge(prod_ready, 2 * g + 2)
                if valid(g - 1, GROUPS) or c == 2:
                    pe.wait_ge(pT_ready, 3 * g + c - 1)
                a, e = CHUNKS[c]
                for j in range(J):
                    ins = nc.tensor.transpose(t_ps[(3 * u + c) % 2][0:ROWS[c], j * P:(j + 1) * P],
                                              prod[:, u % 2, j, a:e], ident)
                ins.then_inc(prod_turned, 1)

            def outputs(g, u, m):
                if not valid(g, GROUPS):
                    return
                if m == 0:
                    pe.wait_ge(pT_ready, 3 * g + 3)
                if isinstance(g, int) and g == 0:
                    pe.wait_ge(skip_ready, SKIP_PAIRS)
                if valid(g - 1, GROUPS):
                    pe.wait_ge(out_copied, 2 * g + m - 1)
                for q in range(2):
                    cols = slice((2 * m + q) * P, (2 * m + q + 1) * P)
                    base = q * OUTS
                    for c, (wc, oc, n) in enumerate(((W_MA, 0, SO), (W_MB, SO + V, 3 * V), (W_MC, SO, 3 * V))):
                        ins = nc.tensor.matmul(o_ps[m][:, base + oc:base + oc + n], pT[c][u % 2][:, cols],
                                               w[0:ROWS[c], wc:wc + n], start=(q == 0 and c == 0),
                                               stop=(q == 1 and c == 2), skip_group_check=True)
                ins.then_inc(out_done, 1)

            def merge(g, u, m):
                if not valid(g, GROUPS):
                    return
                pe.wait_ge(msg_ready, 2 * g + m + 1)
                if m == 0:
                    pe.wait_ge(same_ready, g + 1)
                if valid(g - 1, GROUPS) or m == 1:
                    pe.wait_ge(sums_ready, 2 * g + m)
                for q in range(2):
                    ins = nc.tensor.matmul(d_ps[:, q * M:(q + 1) * M], same[:, u % 2, 2 * m + q, :],
                                           msg[:, u % 2, 2 * m + q, 0:M], start=(q == 0), stop=(q == 1),
                                           skip_group_check=True)
                ins.then_inc(summed, 1)

            def step(i, u):
                g = UNROLL * i + u
                u1, u2, u3 = (u - 1) % UNROLL, (u - 2) % UNROLL, (u - 3) % UNROLL
                turn(g - 1, u1, 0)
                fc2(g, u, 0, 2 * i + u // 2)
                outputs(g - 2, u2, 0)
                turn(g - 1, u1, 1)
                fc2(g, u, 1, 2 * i + u // 2)
                merge(g - 3, u3, 0)
                outputs(g - 2, u2, 1)
                turn(g - 1, u1, 2)
                if u % 2 == 1:
                    fc1(2 * i + u // 2 + 1, (u // 2 + 1) % 2, i + u // 3)
                merge(g - 3, u3, 1)
                if isinstance(g, int) and g == 0:
                    for n in range(SKIP_PAIRS):
                        skip_products(n)

            fc1(0, 0, 0)
            for u in range(UNROLL * PEEL):
                step(u // UNROLL, u % UNROLL)
            with pe.Fori(PEEL, GROUPS // UNROLL - 1) as i:
                for u in range(UNROLL):
                    step(i, u)
            for u in range(UNROLL + TAIL - 1):
                step(GROUPS // UNROLL - 1 + u // UNROLL, u % UNROLL)

        @block.scalar
        def _(act):
            act.wait_ge(eps_set, 1)
            nc.scalar.activation(eps[:, 1:2], eps[:, 0:1], ACT.Sqrt)

            def deviation(n):
                first, end = SCALES[n]
                tt = slice(first * CH, end * CH)
                act.wait_ge(stats_ready, end)
                nc.scalar.activation(node_std[:, 0, tt], mean_var[:, tt, 1], ACT.Sqrt,
                                     bias=eps[:, 0:1]).then_inc(std_ready, 1)

            def copy_node(t):
                act.wait_ge(turned, t + 1)
                nc.scalar.activation(hT[0:3 * V, t, :, :],
                                     t_ps[t % 2][0:3 * V, 0:2 * P].rearrange("p (a b) -> p a b", a=2),
                                     ACT.Copy).then_inc(turned_sb, 1)

            def copy_products(t):
                act.wait_ge(projected, t + 1)
                nc.scalar.activation(node_rows[:, t, :], (o_ps + w_ps)[t % 4][:, 0:F], ACT.Copy,
                                     scale=node_std[:, 1, t:t + 1]).then_inc(rows_ready, 1)

            deviation(0)
            for t in range(NT + 1):
                if t < NT:
                    copy_node(t)
                if t == NT // 2:
                    act.wait_ge(sq_ready, 3)
                    nc.scalar.activation(vlen[:, 1, :], vlen[:, 0, :], ACT.Sqrt).then_inc(len_ready, 1)
                for n, (first, end) in enumerate(SCALES):
                    if n > 0 and t == first * CH - 1:
                        deviation(n)
                    if t == first * CH + 1:
                        act.wait_ge(rstd_ready, n + 1)
                if t >= 1:
                    copy_products(t - 1)

            def copy_skip(n):
                act.wait_ge(skip_done, n + 1)
                for q, t in enumerate(range(2 * n, min(2 * n + 2, NT))):
                    ins = nc.scalar.activation(skip[:, t, :], (d_ps, o_ps[0])[n % 2][:, q * M:(q + 1) * M], ACT.Copy,
                                               scale=node_std[:, 1, t:t + 1])
                ins.then_inc(skip_ready, 1)

            later_zeros = ZERO_PARTS[EARLY_ZEROS:]

            def next_zeros(i):
                if isinstance(i, int) and later_zeros:
                    set_zero(act, *later_zeros.pop(0))

            def hidden(b, par):
                if not valid(b, BLOCKS):
                    return
                act.wait_ge(fc1_done, b + 1)
                if valid(b - 2, BLOCKS):
                    act.wait_ge(fc2_done, 4 * b - 4)
                nc.scalar.activation(hid[:, par, :], hid_ps[:], ACT.Relu).then_inc(hid_ready, 1)

            def copy_turned(g, u, c):
                if not valid(g, GROUPS):
                    return
                act.wait_ge(prod_turned, 3 * g + c + 1)
                if valid(g - 2, GROUPS):
                    act.wait_ge(out_done, 2 * g - 2)
                nc.scalar.activation(pT[c][u % 2][:], t_ps[(3 * u + c) % 2][0:ROWS[c], :],
                                     ACT.Copy).then_inc(pT_ready, 1)

            def copy_outputs(g, u, m):
                if not valid(g, GROUPS):
                    return
                act.wait_ge(out_done, 2 * g + m + 1)
                if valid(g - 2, GROUPS):
                    act.wait_ge(summed, 2 * g + m - 3)
                nc.scalar.activation(msg[:, u % 2, 2 * m:2 * m + 2, :],
                                     o_ps[m][:, 0:2 * OUTS].rearrange("p (q o) -> p q o", q=2),
                                     ACT.Copy).then_inc(out_copied, 1)

            def collect(g, u, m):
                if not valid(g, GROUPS):
                    return
                act.wait_ge(summed, 2 * g + m + 1)
                if valid(g - UNROLL, GROUPS):
                    for j in (2 * m, 2 * m + 1):
                        act.wait_ge(added[j], 16 * (g - UNROLL + 1))
                nc.scalar.activation(to_add[:, u, 2 * m:2 * m + 2, :],
                                     d_ps[:, 0:2 * M].rearrange("p (q o) -> p q o", q=2),
                                     ACT.Copy).then_inc(sums_ready, 1)

            def step(i, u):
                g = UNROLL * i + u
                u1, u2, u3 = (u - 1) % UNROLL, (u - 2) % UNROLL, (u - 3) % UNROLL
                copy_turned(g - 1, u1, 0)
                next_zeros(i)
                copy_outputs(g - 2, u2, 0)
                copy_turned(g - 1, u1, 1)
                next_zeros(i)
                collect(g - 3, u3, 0)
                copy_outputs(g - 2, u2, 1)
                copy_turned(g - 1, u1, 2)
                next_zeros(i)
                if u % 2 == 1:
                    hidden(2 * i + u // 2 + 1, (u // 2 + 1) % 2)
                collect(g - 3, u3, 1)
                if isinstance(g, int) and g == 0:
                    for n in range(SKIP_PAIRS):
                        copy_skip(n)
                        if n % 4 == 0:
                            next_zeros(1)

            hidden(0, 0)
            for u in range(UNROLL * PEEL):
                step(u // UNROLL, u % UNROLL)
            with act.Fori(PEEL, GROUPS // UNROLL - 1) as i:
                for u in range(UNROLL):
                    step(i, u)
            for u in range(UNROLL + TAIL - 1):
                step(GROUPS // UNROLL - 1 + u // UNROLL, u % UNROLL)

            for c, tt in enumerate(LAST):
                act.wait_ge(total_ready, c + 1)
                nc.scalar.activation(gates[:, tt, :], part[c][:, 0, 0:tt.stop - tt.start, 0:SO],
                                     ACT.Sigmoid).then_inc(gate_ready, 1)

        @block.vector
        def _(dve):
            nc.vector.memset(eps[:, 0:1], EPS).then_inc(eps_set, 1)

            def statistics(c):
                dve.wait_ge(x_in[c], 16)
                for t in range(c * CH, (c + 1) * CH):
                    ins = nc.vector.bn_stats(bn[:, t, :], x_sb[:, t, :])
                ins.then_inc(small, 1)
                dve.wait_ge(small, small_at(1))
                for t in range(c * CH, (c + 1) * CH):
                    ins = nc.vector.bn_aggr(mean_var[:, t, :], bn[:, t, :])
                ins.then_inc(stats_ready, 1)

            count = [0]

            def small_at(n):
                count[0] += n
                return count[0]

            def refined(root, square, inv, t0, add):
                nc.vector.reciprocal(inv, root).then_inc(small, 1)
                dve.wait_ge(small, small_at(1))
                nc.vector.scalar_tensor_tensor(t0, square, add, inv, ALU.add, ALU.mult).then_inc(small, 1)
                dve.wait_ge(small, small_at(1))
                nc.vector.tensor_tensor(t0, t0, inv, ALU.mult).then_inc(small, 1)
                dve.wait_ge(small, small_at(1))
                nc.vector.tensor_scalar(t0, t0, -0.5, 1.5, ALU.mult, ALU.add).then_inc(small, 1)
                dve.wait_ge(small, small_at(1))
                return nc.vector.tensor_tensor(inv, inv, t0, ALU.mult)

            def center(c):
                dve.wait_ge(stats_ready, c + 1)
                for t in range(c * CH, (c + 1) * CH):
                    ins = nc.vector.tensor_scalar(h_sb[:, t, :], x_sb[:, t, :], mean_var[:, t, 0:1], 0.0,
                                                  ALU.subtract, ALU.max)
                ins.then_inc(centered, 1)

            def inverse(n):
                dve.wait_ge(std_ready, n + 1)
                tt = slice(SCALES[n][0] * CH, SCALES[n][1] * CH)
                refined(node_std[:, 0, tt], mean_var[:, tt, 1], node_std[:, 1, tt], node_std[:, 3, tt],
                        EPS).then_inc(rstd_ready, 1)

            for c in range(STEPS):
                statistics(c)
                center(c)
                for n, (first, end) in enumerate(SCALES):
                    if c + 1 == end:
                        inverse(n)
            dve.wait_ge(len_ready, 1)
            refined(vlen[:, 1, :], vlen[:, 0, :], vlen[:, 3, :], vlen[:, 2, :], 0.0).then_inc(small, 1)
            dve.wait_ge(small, small_at(1))
            for a, n in ((0, 3), (3, 2)):
                ins = nc.vector.tensor_tensor(rhat[:, :, a:a + n], vec[:, :, 0:n],
                                              vlen[:, 3, :].unsqueeze(2).broadcast_to([P, TILES, n]), ALU.mult)
            ins.then_inc(rhat_ready, 1)

            dve.wait_ge(w_in, 16)
            for r0 in range(0, P, V):
                for wc, n, scale in ((W_MA, SO, 1.0), (W_MB, 3 * V, 3 ** 0.5 if r0 < S else 1.0),
                                     (W_MC, 3 * V, 1.0 if r0 < V else 1.5 ** 0.5)):
                    if wc == W_MA and r0 >= SO:
                        continue
                    ins = nc.vector.tensor_scalar(w[r0:r0 + V, wc:wc + n], w[r0:r0 + V, wc:wc + n],
                                                  scale / 32.0, None, ALU.mult)
            ins.then_inc(scaled, 1)
            dve.wait_ge(scaled, 1)
            dve.wait_ge(rhat_ready, 1)

            def vecs(ap, n):
                return ap.rearrange("p j (i k) -> p j i k", i=n)

            def unit(g, a, n):
                return rhat[:, bass.ds(g * J, J), a:a + n].unsqueeze(3).broadcast_to([P, J, n, V])

            def cross_products(g, u, i):
                if not valid(g, GROUPS):
                    return
                dve.wait_ge(gathered[u], 16 * J * (i + 1))
                if valid(g - 1, GROUPS):
                    dve.wait_ge(crossed, g)
                for dst, i0, n, v0, r0 in ((0, 0, 2, 1, 2), (0, 2, 1, 0, 1), (1, 0, 1, 2, 1), (1, 1, 2, 0, 2),
                                           (2, 0, 3, 0, 0)):
                    ins = nc.vector.tensor_tensor(
                        vecs(crs[:, dst, :, i0 * V:(i0 + n) * V], n),
                        vecs(rows[:, u, :, VE + v0 * V:VE + (v0 + n) * V], n),
                        unit(g, r0, n), ALU.mult)
                ins.then_inc(products, 1)

            def cross_sums(g, u):
                if not valid(g, GROUPS):
                    return
                dve.wait_ge(products, g + 1)
                nc.vector.tensor_tensor(rows[:, u, :, CR:G_END], crs[:, 0], crs[:, 1], ALU.subtract)
                nc.vector.tensor_reduce(rows[:, u, :, DOT:SC], crs[:, 2].rearrange("p j (i k) -> p j k i", i=3),
                                        AXX, ALU.add).then_inc(crossed, 1)

            def edge_products(g, u, m):
                if not valid(g, GROUPS):
                    return
                dve.wait_ge(fc2_done, 2 * g + m + 1)
                if m == 0:
                    dve.wait_ge(crossed, g + 1)
                    if valid(g - 2, GROUPS):
                        dve.wait_ge(prod_turned, 3 * g - 3)
                jj = slice(2 * m, 2 * m + 2)
                we = w_ps[m][:, 0:2 * NFC2].rearrange("p (q n) -> p q n", q=2)
                gr, pr = rows[:, u, jj], prod[:, u % 2, jj]
                nc.vector.tensor_tensor(pr[:, :, 0:E_W1], we[:, :, 0:E_W1], gr[:, :, DOT:VE], ALU.mult)
                nc.vector.tensor_tensor(pr[:, :, E_W1:E_V], we[:, :, E_W1:E_V], gr[:, :, SC:VE], ALU.mult)
                for n, (a, b) in enumerate(((VE, CR), (CR, G_END))):
                    ins = nc.vector.tensor_tensor(
                        vecs(pr[:, :, E_V + 3 * V * n:E_V + 3 * V * (n + 1)], 3),
                        we[:, :, E_V + V * n:E_V + V * (n + 1)].unsqueeze(2).broadcast_to([P, 2, 3, V]),
                        vecs(gr[:, :, a:b], 3), ALU.mult)
                ins.then_inc(prod_ready, 1)

            def radial_part(g, u, m):
                if not valid(g, GROUPS):
                    return
                dve.wait_ge(out_copied, 2 * g + m + 1)
                if valid(g - 1, GROUPS):
                    dve.wait_ge(msg_ready, 2 * g + m - 1)
                nc.vector.tensor_tensor(
                    radial[:, m].rearrange("p q (i k) -> p q i k", i=3),
                    msg[:, u % 2, 2 * m:2 * m + 2, Q:OUTS].unsqueeze(2).broadcast_to([P, 2, 3, V]),
                    rhat[:, bass.ds(g * J + 2 * m, 2), 2:5].unsqueeze(3).broadcast_to([P, 2, 3, V]),
                    ALU.mult).then_inc(radial_ready, 1)

            def vectors(g, u, m):
                if not valid(g, GROUPS):
                    return
                dve.wait_ge(radial_ready, 2 * g + m + 1)
                vm = msg[:, u % 2, 2 * m:2 * m + 2, SO:M]
                nc.vector.tensor_tensor(vm, vm, radial[:, m], ALU.add).then_inc(msg_ready, 1)

            def same_nodes(g, u, i):
                if not valid(g, GROUPS):
                    return
                par, h, k = u // 2, u % 2, u % 2
                dve.wait_ge(from_in[par], 32 * (i + 1))
                if valid(g - 2, GROUPS):
                    dve.wait_ge(summed, 2 * g - 2)
                    dve.wait_ge(idx_ready, g - 1)
                for j in range(J):
                    row = from_row[:, par, (h * J + j) * P:(h * J + j + 1) * P]
                    col = from_col[:, par, h * J + j:h * J + j + 1]
                    nc.vector.tensor_scalar(same[:, k, j, :], row, col, None, ALU.is_equal)
                    nc.vector.scalar_tensor_tensor(before[:, k, j, :], row, col, lower, ALU.is_equal, ALU.mult,
                                                   accum_out=key[:, 0, k, j:j + 1])
                nc.vector.tensor_scalar(key[:, 1, k, :], from_col[:, par, h * J:(h + 1) * J], -1.0,
                                        w[:, W_DUMP:W_DUMP + 1], ALU.mult, ALU.add).then_inc(same_ready, 1)

            def repeats(g, u):
                if not valid(g, GROUPS):
                    return
                k = u % 2
                dve.wait_ge(same_ready, g + 1)
                nc.vector.scalar_tensor_tensor(key[:, 2, k, :], key[:, 0, k, :], 0.5, key[:, 1, k, :],
                                               ALU.is_gt, ALU.mult).then_inc(repeats_ready, 1)

            def rows_to_add(g, u):
                if not valid(g, GROUPS):
                    return
                par, h, k = u // 2, u % 2, u % 2
                dve.wait_ge(repeats_ready, g + 1)
                if valid(g - UNROLL, GROUPS):
                    for j in range(J):
                        dve.wait_ge(added[j], 16 * (g - UNROLL + 1))
                nc.vector.tensor_tensor(add_idx[:, u, :], key[:, 2, k, :], from_col[:, par, h * J:(h + 1) * J],
                                        ALU.add).then_inc(idx_ready, 1)

            def step(i, u):
                g = UNROLL * i + u
                u2 = (u - 2) % UNROLL
                nx, ni = (u + 1) % UNROLL, i + (u + 1) // UNROLL
                cross_products(g + 1, nx, ni)
                edge_products(g, u, 0)
                radial_part(g - 2, u2, 0)
                cross_sums(g + 1, nx)
                edge_products(g, u, 1)
                vectors(g - 2, u2, 0)
                early = isinstance(g, int) and g - 2 < EARLY_GROUPS
                if not early:
                    same_nodes(g - 2, u2, i - (1 if u < 2 else 0))
                radial_part(g - 2, u2, 1)
                if not early:
                    repeats(g - 2, u2)
                vectors(g - 2, u2, 1)
                if not early:
                    rows_to_add(g - 2, u2)

            for g in range(EARLY_GROUPS):
                same_nodes(g, g, 0)
                repeats(g, g)
                rows_to_add(g, g)
            cross_products(0, 0, 0)
            cross_sums(0, 0)
            for u in range(UNROLL * PEEL):
                step(u // UNROLL, u % UNROLL)
            with dve.Fori(PEEL, GROUPS // UNROLL - 1) as i:
                for u in range(UNROLL):
                    step(i, u)
            for u in range(UNROLL + TAIL - 2):
                step(GROUPS // UNROLL - 1 + u // UNROLL, u % UNROLL)

            def total(c, tt):
                pc = part[c][:, :, 0:tt.stop - tt.start]
                dve.wait_ge(three_in[c], 16 * 3)
                nc.vector.tensor_tensor(pc[:, 0], pc[:, 0], pc[:, 1], ALU.add).then_inc(pair_sum, 1)
                if c < len(LAST) - 1:
                    dve.wait_ge(half_sum, c + 1)
                    dve.wait_ge(pair_sum, c + 1)
                else:
                    dve.wait_ge(pair_sum, c + 1)
                    dve.wait_ge(fourth_in[c], 16)
                    nc.vector.tensor_tensor(pc[:, 0], pc[:, 0], pc[:, 3], ALU.add).then_inc(pair_sum, 1)
                    dve.wait_ge(pair_sum, c + 2)
                    dve.wait_ge(with_skip, c + 1)
                nc.vector.tensor_tensor(pc[:, 0], pc[:, 0], pc[:, 2], ALU.add).then_inc(total_ready, 1)

            def finish(c, tt):
                n = tt.stop - tt.start
                pc, gt, xt = part[c][:, 0, 0:n], gates[:, tt, :], x_sb[:, tt, :]
                dve.wait_ge(gate_ready, c + 1)
                nc.vector.tensor_tensor(pc[:, :, 0:S], pc[:, :, 0:S], gt[:, :, 0:S], ALU.mult)
                vm = pc[:, :, SO:M].rearrange("p t (i k) -> p t i k", i=3)
                nc.vector.tensor_tensor(vm, vm, gt[:, :, S:SO].unsqueeze(2).broadcast_to([P, n, 3, V]),
                                        ALU.mult).then_inc(gated, 1)
                dve.wait_ge(gated, c + 1)
                nc.vector.tensor_tensor(xt[:, :, 0:S], xt[:, :, 0:S], pc[:, :, 0:S], ALU.add)
                xv = xt[:, :, S:F].rearrange("p t (k i) -> p t i k", i=3)
                nc.vector.tensor_tensor(xv[:, :, 0:2], xv[:, :, 0:2], vm[:, :, 1:3], ALU.add)
                nc.vector.tensor_tensor(xv[:, :, 2], xv[:, :, 2], vm[:, :, 0], ALU.add).then_inc(out_ready, 1)

            for c, tt in enumerate(LAST):
                total(c, tt)
                if c >= 1:
                    finish(c - 1, LAST[c - 1])
            finish(len(LAST) - 1, LAST[-1])


def pack_weights(skip0, skip1, nl0, nl1, fc1, fc2, out_s, out_v):
    w = np.zeros((P, W_END), np.float32)

    def put(r, c, a):
        w[r:r + a.shape[0], c:c + a.shape[1]] = a

    for h in range(2):
        put(FE * h, W_FC1 + FE * h, fc1)
        c = W_FC2
        w0, w1, w2, w3, w4 = fc2[:, 0:64], fc2[:, 64:128], fc2[:, 128:160], fc2[:, 160:192], fc2[:, 192:224]
        for a in (w3, w0, w1, w2, w4):
            put(FE * h, c, a)
            c += a.shape[1]
    put(0, W_MA, out_s[S:])
    put(V, W_MA, out_s[:S])
    put(0, W_MB + 2 * V, out_v[0:S])
    put(S, W_MB, out_v[S:S + V])
    put(S + V, W_MB + V, out_v[S:S + V])
    put(0, W_MC, out_v[S:S + V])
    for i in range(3):
        put(V + i * V, W_MC + (i + 1) % 3 * V, out_v[S + V:])
        w[i:3 * V:3, W_NV + i * V:W_NV + (i + 1) * V] = nl1
        w[i:3 * V:3, W_NV + (3 + (i + 1) % 3) * V:W_NV + (4 + (i + 1) % 3) * V] = skip1
    put(0, W_NS, skip0)
    put(0, W_NS + SO, nl0)
    put(0, W_ID, np.eye(P, dtype=np.float32))
    put(0, W_LT, np.tril(np.ones((P, P), np.float32), -1))
    w[:, W_DUMP] = NPAD + np.arange(P)
    return w


def kernel(x, src, dst, edge_attr_3, edge_attr_64, L0_gnn_W_skip0, L0_gnn_W_skip1, L0_gnn_W_nl0, L0_gnn_W_nl1,
           L0_gnn_W_fc1, L0_gnn_W_fc2, L0_gnn_W_out_s, L0_gnn_W_out_v):
    import concourse.bacc as bacc
    from concourse.bass_utils import run_bass_kernel_spmd

    def padded(a, n, fill=0):
        a = np.asarray(a)
        rest = np.full((n - a.shape[0],) + a.shape[1:], fill, a.dtype)
        return np.concatenate([a, rest])

    def in_blocks(a):
        tiles = padded(a, TILES * P, 1 if a.ndim == 2 else 0).reshape(2, BLOCKS, J, P, -1)
        return np.ascontiguousarray(tiles.transpose(1, 0, 2, 3, 4)).reshape(TILES, P, -1)

    src, dst = np.asarray(src), np.asarray(dst)
    ea = np.asarray(edge_attr_3)
    ef = padded(edge_attr_64, TILES * P).reshape(2, HALF * P, FE).transpose(0, 2, 1).reshape(2 * FE, HALF * P)
    arrays = {
        "x": padded(x, NPAD),
        "wpack": pack_weights(*(np.asarray(a) for a in (
            L0_gnn_W_skip0, L0_gnn_W_skip1, L0_gnn_W_nl0, L0_gnn_W_nl1, L0_gnn_W_fc1, L0_gnn_W_fc2,
            L0_gnn_W_out_s, L0_gnn_W_out_v))),
        "edge_t": np.ascontiguousarray(ef),
        "nodes_to": np.ascontiguousarray(in_blocks(dst)[:, :, 0].T),
        "nodes_from": np.ascontiguousarray(in_blocks(src)[:, :, 0].T),
        "nodes_row": np.ascontiguousarray(in_blocks(src).reshape(1, TILES * P)),
        "edge_vec": np.ascontiguousarray(in_blocks(ea).transpose(1, 0, 2)),
    }
    nc = bacc.Bacc("TRN2", target_bir_lowering=False, num_devices=1)
    aps = {n: nc.dram_tensor(n, a.shape, mybir.dt.from_np(a.dtype), kind="ExternalInput").ap()
           for n, a in arrays.items()}
    out = nc.dram_tensor("out", (NPAD, F), F32, kind="ExternalOutput").ap()
    build_program(nc, out=out, **aps)
    r = run_bass_kernel_spmd(nc, [arrays], core_ids=[0])
    return r.results[0]["out"][:N]
```
